# Optimizing a Trainium2 kernel written in Bass

```python
import numpy as np
import jax
import jax.numpy as jnp

def _softmax(x, axis=-1):
    return jax.nn.softmax(x, axis=axis)

def _gelu(x):
    return jax.nn.gelu(x, approximate=True)

def _silu(x):
    return jax.nn.silu(x)

def _sigmoid(x):
    return jax.nn.sigmoid(x)

def _layernorm(x, axis=-1, eps=1e-05):
    m = jnp.mean(x, axis=axis, keepdims=True)
    v = jnp.var(x, axis=axis, keepdims=True)
    return (x - m) / jnp.sqrt(v + eps)

def _scatter_add(tgt, idx, src, axis=0):
    return tgt.at[idx].add(src)

def _segment_sum(src, seg, n):
    return jax.ops.segment_sum(src, seg, n)
kernel_name = 'mk_gnn_resnorm_d1_gnn_r8_773865'

def setup_inputs(seed: int=0):
    np.random.seed(seed)
    _w = jnp.asarray

    def _rec_inputs():
        import jax
        import jax.numpy as jnp
        _gk = jax.random.key(seed)
        x = -0.0003713 + 1 * jax.random.normal(jax.random.fold_in(_gk, 1), (12500, 256), jnp.float32)
        src = jax.random.randint(jax.random.fold_in(_gk, 2), (200000,), 0, 12500, jnp.int32)
        dst = jax.random.randint(jax.random.fold_in(_gk, 3), (200000,), 0, 12500, jnp.int32)
        _o = jnp.argsort(dst, stable=True)
        src = src[_o]
        dst = dst[_o]
        edge_weight = jax.random.uniform(jax.random.fold_in(_gk, 12), (200000,), jnp.float32, 0.0, 0.999998)
        return (x, src, dst, edge_weight)
    x, src, dst, edge_weight = _rec_inputs()

    def _L0_gnn_setup():
        import jax, jax.numpy as jnp
        import numpy as np
        N_NODES = 6250
        N_EDGES = 100000
        IN_DIM, HID_DIM, OUT_DIM, N_HEADS = (256, 256, 64, 4)
        ATT_DIM = OUT_DIM * 2 + 1
        key = jax.random.key(seed)
        ks = jax.random.split(key, 8)
        s = 0.05
        return {'x': jax.random.normal(ks[0], (N_NODES, IN_DIM), dtype=jnp.float32), 'idx': jax.random.randint(ks[1], (2, N_EDGES), 0, N_NODES, dtype=jnp.int32), 'elem': jax.random.uniform(ks[2], (N_EDGES,), dtype=jnp.float32), 'W1': jax.random.normal(ks[3], (N_HEADS, IN_DIM, HID_DIM), dtype=jnp.float32) * s, 'b1': jnp.zeros((N_HEADS, HID_DIM), jnp.float32), 'W2': jax.random.normal(ks[4], (N_HEADS, HID_DIM, OUT_DIM), dtype=jnp.float32) * s, 'b2': jnp.zeros((N_HEADS, OUT_DIM), jnp.float32), 'A1': jax.random.normal(ks[5], (N_HEADS, ATT_DIM, ATT_DIM), dtype=jnp.float32) * s, 'ab1': jnp.zeros((N_HEADS, ATT_DIM), jnp.float32), 'A2': jax.random.normal(ks[6], (N_HEADS, ATT_DIM, 1), dtype=jnp.float32) * s, 'ab2': jnp.zeros((N_HEADS, 1), jnp.float32)}
    _L0_gnn_all = _L0_gnn_setup()
    _L0_gnn_in = {k: v for k, v in _L0_gnn_all.items() if k in ('W1', 'b1', 'W2', 'b2', 'A1', 'ab1', 'A2', 'ab2')}
    del _L0_gnn_all
    return {'x': x, 'src': src, 'dst': dst, 'edge_weight': edge_weight, 'L0_gnn_W1': _L0_gnn_in['W1'], 'L0_gnn_b1': _L0_gnn_in['b1'], 'L0_gnn_W2': _L0_gnn_in['W2'], 'L0_gnn_b2': _L0_gnn_in['b2'], 'L0_gnn_A1': _L0_gnn_in['A1'], 'L0_gnn_ab1': _L0_gnn_in['ab1'], 'L0_gnn_A2': _L0_gnn_in['A2'], 'L0_gnn_ab2': _L0_gnn_in['ab2']}

def reference(x, src, dst, edge_weight, L0_gnn_W1, L0_gnn_b1, L0_gnn_W2, L0_gnn_b2, L0_gnn_A1, L0_gnn_ab1, L0_gnn_A2, L0_gnn_ab2):
    import jax
    import jax.numpy as jnp

    def _L0_gnn_ref(x, idx, elem, W1, b1, W2, b2, A1, ab1, A2, ab2):
        import jax, jax.numpy as jnp
        import numpy as np
        N_NODES = 6250
        N_EDGES = 100000
        IN_DIM, HID_DIM, OUT_DIM, N_HEADS = (256, 256, 64, 4)
        ATT_DIM = OUT_DIM * 2 + 1
        row, col = (idx[0], idx[1])
        n = x.shape[0]

        def head(w1, bb1, w2, bb2, a1, aab1, a2, aab2):
            feats = jnp.maximum(x @ w1 + bb1, 0.0) @ w2 + bb2
            x_cat = jnp.concatenate([feats[row], feats[col], elem[:, None]], axis=1)
            hid = jnp.maximum(x_cat @ a1 + aab1, 0.0)
            e1 = (hid @ a2 + aab2)[:, 0]
            e1 = jax.nn.leaky_relu(e1, negative_slope=0.2)
            w = jnp.exp(e1 - jnp.max(e1))
            pooled = jax.ops.segment_sum(w[:, None] * feats[col], row, num_segments=n)
            row_sum = jax.ops.segment_sum(w, row, num_segments=n) + 1e-10
            return pooled / row_sum[:, None]
        h = jax.vmap(head)(W1, b1, W2, b2, A1, ab1, A2, ab2)
        return jnp.transpose(h, (1, 0, 2)).reshape(n, -1)
    edge_index = jnp.stack([src, dst])
    x = _layernorm(x + _L0_gnn_ref(x, edge_index, edge_weight, L0_gnn_W1, L0_gnn_b1, L0_gnn_W2, L0_gnn_b2, L0_gnn_A1, L0_gnn_ab1, L0_gnn_A2, L0_gnn_ab2), axis=-1)
    return x

_drawn_inputs = setup_inputs


def setup_inputs(seed=0):
    import zlib

    import numpy as np

    out = dict(_drawn_inputs(seed))
    spreads = {'L0_gnn_b1': (0.0, 0.1),
     'L0_gnn_b2': (0.0, 0.1),
     'L0_gnn_ab1': (0.0, 0.8),
     'L0_gnn_ab2': (0.0, 2.0)}
    factors = {'edge_weight': 8.0, 'L0_gnn_A1': 8.0, 'L0_gnn_A2': 8.0}
    for name, (base, spread) in spreads.items():
        noise = np.random.default_rng([zlib.crc32(name.encode()), seed]).standard_normal(out[name].shape)
        drawn = base * np.exp(spread * noise) if base else spread * noise
        out[name] = jnp.asarray(drawn.astype(out[name].dtype))
    for name, factor in factors.items():
        out[name] = (out[name] * factor).astype(out[name].dtype)
    return out
```

```python
from contextlib import ExitStack

import concourse.bass as bass
from concourse import mybir

ALU = mybir.AluOpType
ACT = mybir.ActivationFunctionType
F32 = mybir.dt.float32
I32 = mybir.dt.int32
BF16 = mybir.dt.bfloat16
AX_X = mybir.AxisListType.X


def gnn_layer(nc, x, src, dst, weight, W1, b1, W2, b2, A1, ab1, A2, ab2, out):
    N, D = x.shape
    E = src.shape[0]
    H, _, HID = W1.shape
    DO = W2.shape[2]
    AT = 2 * DO + 1
    P = 128
    WN = 125
    W = N // WN
    GROUPS = W // 4
    EP = 125
    EC = E // EP
    CPI = EC // GROUPS
    SUBS = 4
    LOT = CPI // SUBS
    CH = 4
    CHUNKS = LOT // CH
    assert N == WN * W and E == EP * EC and CPI * GROUPS == EC and CHUNKS * CH * SUBS == CPI
    ZW = H * AT
    HF = DO + 1
    QW = ZW + H * HF
    HALF = 2 * AT
    SB = 4
    RING = 16
    SPB = RING // SB
    NT = (E + W * (P - 1)) // P
    NT = -(-NT // RING) * RING
    NSB = NT // SB
    BODIES = NT // RING
    KC = D // P
    MC = H * HID // P
    NG = 4 * WN
    EPS = 1e-5
    LOW = -1e30

    qf_table = nc.dram_tensor("qf_table", (N, QW), F32, kind="Internal").ap()
    p_table = nc.dram_tensor("p_table", (N, 3 * ZW), BF16, kind="Internal").ap()
    records = nc.dram_tensor("records", (P * NT, 4), F32, kind="Internal").ap()

    ctx = ExitStack()
    with ctx:
        def sb(name, shape, dt=F32):
            return ctx.enter_context(nc.sbuf_tensor(name, shape, dt))

        def sem(name):
            return ctx.enter_context(nc.semaphore(name))

        acc = sb("acc", [P, max(W * H * HF, 22400)])
        z = sb("z", [P, RING * QW])
        rec_all = sb("rec_all", [P, NT * 4])
        p_win = sb("p_win", [P, 2, 3 * ZW], BF16)
        ident = sb("ident", [P, P])
        ones_f = sb("ones_f", [P, P])
        ones_b = sb("ones_b", [P, P], BF16)
        before = sb("before", [P, P], BF16)
        iota_row = sb("iota_row", [P, WN])
        iota_win = sb("iota_win", [P, CH, W], BF16)
        a2_b = sb("a2_b", [P, ZW])
        ab2_b = sb("ab2_b", [P, H])
        onehot = sb("onehot", [P, RING, P])
        onehot_t = sb("onehot_t", [P, RING // 2, P], BF16)
        rec = sb("rec", [P, RING, 4])
        e_raw = sb("e_raw", [P, RING, H])
        e_val = sb("e_val", [P, RING, H])
        tile_max = sb("tile_max", [P, SPB, H])
        head_max = sb("head_max", [H, SPB])
        max_diag = sb("max_diag", [H, SPB, H])
        shift = sb("shift", [P, SPB, H])
        e_sh = sb("e_sh", [P, RING, H])
        drop = sb("drop", [P, SPB, H])
        decay = sb("decay", [P, SPB, H])
        shift_all = sb("shift_all", [P, NSB, H])
        end_tiles = sb("end_tiles", [1, W], I32)
        last_sb = sb("last_sb", [1, W], I32)
        end_prev = sb("end_prev", [1, W], I32)
        win_pack = sb("win_pack", [1, NSB], I32)
        psum = ctx.enter_context(nc.psum_tensor("psum", [P, 8, 512], F32))

        win_of = onehot[0:1, :, :].rearrange("p t n -> p (t n)").bitcast(I32)[:, 0:NT]
        row_tmp = onehot_t[0:1, :, :].rearrange("p t n -> p (t n)").bitcast(I32)[:, 0:NSB]
        assert NT <= RING * P
        used = [0]

        def carve(n):
            used[0] += n
            return acc[:, used[0] - n:used[0]]

        w1_s = carve(KC * H * HID).rearrange("p (k h n) -> p k h n", k=KC, h=H)
        w2_s = carve(MC * P).rearrange("p (m n) -> p m n", m=MC)
        ad_s = carve(2 * 2 * HALF).rearrange("p (q u n) -> p q u n", q=2, u=2)
        ab1_b = carve(ZW)
        b1_s = carve(MC)
        b2_s = carve(2)
        x_rows = carve(4 * D).rearrange("p (w n) -> p w n", w=4)
        x_t = carve(KC * NG).rearrange("p (k n) -> p k n", k=KC)
        h_t = carve(MC * NG).rearrange("p (m n) -> p m n", m=MC)
        f_t = carve(2 * NG).rearrange("p (q n) -> p q n", q=2)
        p_f = carve(ZW)
        p_out = carve(2 * 3 * ZW // 2).bitcast(BF16).rearrange("p (b n) -> p b n", b=2)
        qf_out = carve(2 * QW).rearrange("p (b n) -> p b n", b=2)
        assert used[0] <= 16000
        a_row = carve(ZW)
        a_rest = carve(ZW)
        a_parts = carve(3 * ZW // 2 + 2).bitcast(BF16)[:, 0:3 * ZW]
        src_i = carve(EC).bitcast(I32)
        dst_i = carve(EC).bitcast(I32)
        tmp_a = carve(EC)
        assert used[0] <= 22400
        used_z = [0]

        def carve_z(n):
            used_z[0] += n
            return z[:, used_z[0] - n:used_z[0]]

        rec_src = carve_z(EC * 4)
        edge_win = carve_z(EC // 2).bitcast(BF16)
        win_oh = carve_z(2 * CH * W // 2).bitcast(BF16).rearrange("p (b c w) -> p b c w", b=2, c=CH)
        count_t = carve_z(2 * (CH + 1) * W).rearrange("p (b n) -> p b n", b=2)
        pos_f = carve_z(SUBS * LOT).rearrange("p (s n) -> p s n", s=SUBS)
        pos_i = carve_z(SUBS * LOT).bitcast(I32).rearrange("p (s n) -> p s n", s=SUBS)
        pos_p = carve_z(LOT).bitcast(I32)
        pos_t = carve_z(LOT).bitcast(I32)
        pos_at = carve_z(SUBS * LOT).bitcast(I32).rearrange("p (s n) -> p s n", s=SUBS)
        rec_out = carve_z(SUBS * LOT * 4).rearrange("p (s n) -> p s n", s=SUBS)
        win_iota = carve_z(NT)
        counts = carve_z(W)
        sizes_i = carve_z(W).bitcast(I32)
        sizes = carve_z(W)
        ends = carve_z(W)
        end_col = carve_z(1)
        zeros_b = carve_z(P // 2 + 1).bitcast(BF16)[:, 0:P]
        win_done = carve_z(NT // 2).bitcast(BF16)
        assert used_z[0] <= RING * QW
        weight_f = rec_all[:, 0:EC]
        empty = p_win[:, :, :].rearrange("p a n -> p (a n)").bitcast(F32)[:, 0:SB * 4 * 16]

        p_flat = p_win[:, :, :].rearrange("p a n -> p (a n)")
        shift_flat = shift_all[:, :, :].rearrange("p s h -> p (s h)")
        z_t = z[:, :].rearrange("p (t n) -> p t n", t=RING)
        acc_w = acc[:, 0:W * H * HF].rearrange("p (w n) -> p w n", w=W)
        rec_words = rec_all[:, :].rearrange("p (t n) -> p t n", n=4)

        s_const = sem("s_const")
        s_weights = sem("s_weights")
        s_edges = sem("s_edges")
        s_edge_step = sem("s_edge_step")
        s_a_step = sem("s_a_step")
        s_a_rows = sem("s_a_rows")
        s_empty = sem("s_empty")
        s_hist_oh = sem("s_hist_oh")
        s_hist = sem("s_hist")
        s_base = sem("s_base")
        s_tab_mm = sem("s_tab_mm")
        s_tab_step = sem("s_tab_step")
        s_acc_zero = sem("s_acc_zero")
        s_passed = sem("s_passed")
        s_passed_c = sem("s_passed_c")
        s_x = sem("s_x")
        s_xt_mm = sem("s_xt_mm")
        s_xt = sem("s_xt")
        s_h_mm = sem("s_h_mm")
        s_h_ev = sem("s_h_ev")
        s_f_mm = sem("s_f_mm")
        s_f_ev = sem("s_f_ev")
        s_p_mm = sem("s_p_mm")
        s_p_ev = sem("s_p_ev")
        s_p_hi = sem("s_p_hi")
        s_p_rest = sem("s_p_rest")
        s_p_mid = sem("s_p_mid")
        s_p_lo = sem("s_p_lo")
        s_t_mm = sem("s_t_mm")
        s_t_ev = sem("s_t_ev")
        s_q_mm = sem("s_q_mm")
        s_q_ev = sem("s_q_ev")
        s_p_st = [sem(f"s_p_st{n}") for n in range(2)]
        s_qf_st = [sem(f"s_qf_st{n}") for n in range(2)]
        s_oh = sem("s_oh")
        s_count = sem("s_count")
        s_carry = sem("s_carry")
        s_pos = sem("s_pos")
        s_at = sem("s_at")
        s_scat = [sem(f"s_scat{n}") for n in range(SUBS)]
        s_rec_all = sem("s_rec_all")
        s_start = sem("s_start")
        s_win = [sem(f"s_win{n}") for n in range(2)]
        s_win_ready = sem("s_win_ready")
        s_rec = sem("s_rec")
        s_onehot = sem("s_onehot")
        s_oht_mm = sem("s_oht_mm")
        s_oht = sem("s_oht")
        s_z_mm = sem("s_z_mm")
        s_z_ev = sem("s_z_ev")
        s_z_zero = sem("s_z_zero")
        s_gather = [sem(f"s_gather{n}") for n in range(RING)]
        s_dot = sem("s_dot")
        s_e_bias = sem("s_e_bias")
        s_e_leaky = sem("s_e_leaky")
        s_e_mask = sem("s_e_mask")
        s_head_max = sem("s_head_max")
        s_drop = sem("s_drop")
        s_decay = sem("s_decay")
        s_decayed = sem("s_decayed")
        s_shift_all = sem("s_shift_all")
        s_tmax = sem("s_tmax")
        s_tmax_t = sem("s_tmax_t")
        s_diag = sem("s_diag")
        s_max_b = sem("s_max_b")
        s_shift = sem("s_shift")
        s_esh = sem("s_esh")
        s_w = sem("s_w")
        s_wf = sem("s_wf")
        s_agg = sem("s_agg")
        s_acc = sem("s_acc")
        s_c_x = sem("s_c_x")
        s_c = sem("s_c")
        s_c_exp = sem("s_c_exp")
        s_c_y = sem("s_c_y")
        s_c_std = sem("s_c_std")
        s_c_out = sem("s_c_out")
        s_c_ready = sem("s_c_ready")

        CG = 4
        c_x = z[:, 0:CG * D].rearrange("p (w n) -> p w n", w=CG)
        c_y = z[:, CG * D:2 * CG * D].rearrange("p (w n) -> p w n", w=CG)
        c_o = z[:, 2 * CG * D:3 * CG * D].rearrange("p (w n) -> p w n", w=CG)
        c_s = rec_all[:, 0:CG * H].rearrange("p (w h) -> p w h", w=CG)
        c_e = rec_all[:, 16:16 + CG * H].rearrange("p (w h) -> p w h", w=CG)
        c_d = rec_all[:, 32:32 + CG * H].rearrange("p (w h) -> p w h", w=CG)
        c_r = rec_all[:, 48:48 + CG * H].rearrange("p (w h) -> p w h", w=CG)
        c_k = rec_all[:, 64:64 + CG * H].rearrange("p (w h) -> p w h", w=CG)
        c_st = rec_all[:, 80:80 + CG * 6].rearrange("p (w h) -> p w h", w=CG)
        c_mv = rec_all[:, 104:104 + CG * 2].rearrange("p (w h) -> p w h", w=CG)
        c_sd = rec_all[:, 112:112 + CG]
        c_is = rec_all[:, 116:116 + CG]
        c_eps = rec_all[:, 120:121]

        block = ctx.enter_context(nc.Block())

        N_W = 16 * (KC + MC + 2 * H + 5 + 2)
        N_EMPTY = -(-NT * 4 // (SB * 4 * 16))
        N_TAB = -(-NT // 512)
        C_VAR = 3 * CG + 5
        C_STEPS = C_VAR + 1

        def live(i, k, off):
            return not isinstance(i, int) or 0 <= i * SPB + k + off < NSB

        def since(eng, semaphore, count):
            if not (isinstance(count, int) and count <= 0):
                eng.wait_ge(semaphore, count)

        def loop(eng, n, body):
            body(0)
            with eng.Fori(1, n) as g:
                body(g)

        def group_at(g):
            return slice(g, g + 1) if isinstance(g, int) else bass.ds(g, 1)

        def win_at(pack, j):
            return nc.s_assert_within((pack // (1 << 7 * j)) % 128 if j else pack % 128, 0, W - 1,
                                      skip_runtime_bounds_check_because="the table is clipped at W - 1")

        WEIGHTED = [(-2, 2), (-2, 3), (-1, 0), (-1, 1)]

        def pipeline(eng, step):
            step(-1, 2)
            step(-1, 3)
            for k in range(SPB):
                step(0, k)
            with eng.Fori(1, BODIES - 1) as i:
                for k in range(SPB):
                    step(i, k)
            for k in range(SPB):
                step(BODIES - 1, k)
            step(BODIES, 0)
            step(BODIES, 1)


        @block.sync
        def _(sp):
            sp.dma_start(src_i[0:EP, :], src.rearrange("(p c) -> p c", p=EP)).then_inc(s_edges, 16)
            sp.dma_start(weight_f[0:EP, :], weight.rearrange("(p c) -> p c", p=EP)).then_inc(s_edges, 16)
            sp.dma_start(dst_i[0:EP, :], dst.rearrange("(p c) -> p c", p=EP)).then_inc(s_edges, 16)
            for k in range(KC):
                sp.dma_start(w1_s[:, k, :, :], W1[:, k * P:(k + 1) * P, :].rearrange("h p n -> p h n")).then_inc(s_weights, 16)
            sp.wait_ge(s_const, 2)
            for m in range(MC):
                h, c = m // (HID // P), m % (HID // P)
                sp.dma_start(w2_s[:, m, (h % 2) * DO:(h % 2 + 1) * DO], W2[h, c * P:(c + 1) * P, :]).then_inc(s_weights, 16)
            for h in range(H):
                for u in range(2):
                    sp.dma_start(ad_s[(h % 2) * DO:(h % 2 + 1) * DO, h // 2, u, (h % 2) * AT:(h % 2 + 1) * AT],
                                 A1[h, u * DO:(u + 1) * DO, :]).then_inc(s_weights, 16)
            sp.dma_start(ab1_b, ab1.rearrange("(a h) n -> a (h n)", a=1).to_broadcast([P, ZW])).then_inc(s_weights, 16)
            sp.dma_start(a2_b[:, :], A2.rearrange("(a h) n b -> a (h n b)", a=1).to_broadcast([P, ZW])).then_inc(s_weights, 16)
            sp.dma_start(ab2_b[:, :], ab2.rearrange("(a h) n -> a (h n)", a=1).to_broadcast([P, H])).then_inc(s_weights, 16)
            sp.dma_start(a_row[0:1, :], A1[:, 2 * DO, :].rearrange("(a h) n -> a h n", a=1)).then_inc(s_weights, 16)
            sp.dma_start(b1_s, b1.rearrange("h (c p) -> p (h c)", p=P), allow_slow_non_contiguous=True).then_inc(s_weights, 16)
            for q in range(2):
                sp.dma_start(b2_s[:, q:q + 1], b2[2 * q:2 * q + 2, :].rearrange("r (d a) -> (r d) a", a=1),
                             allow_slow_non_contiguous=True).then_inc(s_weights, 16)
            sp.wait_ge(s_empty, 1)
            EW = SB * 4 * 16
            flat = records.rearrange("(p t) n -> p (t n)", p=P)
            for o in range(0, NT * 4, EW):
                n = min(EW, NT * 4 - o)
                sp.dma_start(flat[:, o:o + n], empty[:, 0:n]).then_inc(s_empty, 16)
            x_g = x.rearrange("(g w p) n -> g p w n", w=4, p=WN)
            p_g = p_table.rearrange("(g w p) n -> g w p n", w=4, p=WN)
            qf_g = qf_table.rearrange("(g w p) n -> g w p n", w=4, p=WN)

            def load_x(g):
                since(sp, s_xt_mm, g)
                sp.dma_start(x_rows[0:WN, :, :], x_g[group_at(g), :, :, :].rearrange("a p w n -> (a p) w n")).then_inc(s_x, 16)

            def store(g):
                for w in range(4):
                    sp.wait_ge(s_p_lo, g * 4 + w + 1)
                    sp.dma_start(p_g[group_at(g), w, :, :].rearrange("a p n -> (a p) n"), p_out[0:WN, w % 2, :]).then_inc(s_p_st[w % 2], 16)
                    sp.wait_ge(s_q_ev, g * 4 + w + 1)
                    sp.wait_ge(s_t_ev, g * 4 + w + 1)
                    sp.dma_start(qf_g[group_at(g), w, :, :].rearrange("a p n -> (a p) n"), qf_out[0:WN, w % 2, :]).then_inc(s_qf_st[w % 2], 16)

            def group(g):
                load_x(g + 1)
                store(g)

            load_x(0)
            loop(sp, GROUPS - 1, group)
            store(GROUPS - 1)
            for n in range(2):
                sp.wait_ge(s_p_st[n], 32 * GROUPS)
                sp.wait_ge(s_qf_st[n], 32 * GROUPS)
            for n in range(SUBS):
                sp.wait_ge(s_scat[n], 16 * LOT * GROUPS)
            sp.wait_ge(s_a_step, 5)
            for slot in range(2):
                for r in range(3):
                    sp.dma_start(p_win[WN + r:WN + r + 1, slot, :], a_parts[0:1, :]).then_inc(s_a_rows, 16)
            sp.dma_start(rec_all[:, :], records.rearrange("(p t) n -> p (t n)", p=P)).then_inc(s_rec_all, 16)
            sp.wait_ge(s_a_rows, 16 * 6)
            sp.wait_ge(s_rec_all, 16)
            sp.sem_inc(s_start, 1)
            p_w = p_table.rearrange("(g v p) n -> g v p n", v=2, p=WN)
            with sp.Fori(0, W // 2) as g:
                for v in range(2):
                    done = sp.value_load(end_prev[0:1, bass.ds(g * 2 + v, 1)], min_val=1, max_val=NT + 1)
                    sp.wait_ge(s_z_mm, done)
                    sp.dma_start(p_win[0:WN, v, :], p_w[bass.ds(g, 1), v, :, :].rearrange("a p n -> (a p) n")).then_inc(s_win[v], 16)
                    sp.wait_ge(s_win[v], g * 16 + 16)
                    sp.sem_inc(s_win_ready, 1)
            x_c = x.rearrange("(g w p) n -> g p w n", w=CG, p=WN)
            o_c = out.rearrange("(g w p) n -> g p w n", w=CG, p=WN)
            sp.wait_ge(s_acc, NT)
            def finish(g):
                since(sp, s_c_y, g)
                sp.dma_start(c_x[0:WN, :, :], x_c[group_at(g), :, :, :].rearrange("a p w n -> (a p) w n")).then_inc(s_c_x, 16)
                sp.wait_ge(s_c_ready, g + 1)
                sp.dma_start(o_c[group_at(g), :, :, :].rearrange("a p w n -> (a p) w n"), c_o[0:WN, :, :]).then_inc(s_c_out, 16)
            loop(sp, W // CG, finish)
            sp.wait_ge(s_c_out, 16 * (W // CG))

        @block.gpsimd
        def _(pool):
            pool.memset(w2_s, 0.0).then_inc(s_const, 1)
            pool.memset(ad_s, 0.0).then_inc(s_const, 1)
            rec_w = empty.rearrange("p (t n) -> p t n", n=4)
            pool.memset(empty, 0.0).then_inc(s_const, 1)
            pool.wait_ge(s_const, 3)
            pool.memset(rec_w[:, :, 2:3].bitcast(BF16)[:, :, 1:2], LOW).then_inc(s_empty, 1)
            pool.memset(ones_f[:, :], 1.0).then_inc(s_const, 1)
            pool.memset(ones_b[:, :], 1.0).then_inc(s_const, 1)
            pool.memset(ident[:, :], 0.0).then_inc(s_const, 1)
            pool.memset(qf_out, 0.0).then_inc(s_const, 1)
            pool.memset(zeros_b, 0.0).then_inc(s_const, 1)
            pool.iota(iota_row[:, :], [[1, WN]], base=1, channel_multiplier=0, allow_small_or_imprecise_dtypes=True).then_inc(s_const, 1)
            pool.iota(iota_win[:, :, :], [[0, CH], [1, W]], base=0, channel_multiplier=0, allow_small_or_imprecise_dtypes=True).then_inc(s_const, 1)
            pool.iota(win_iota, [[P, NT]], base=0, channel_multiplier=0, allow_small_or_imprecise_dtypes=True).then_inc(s_const, 1)
            pool.wait_ge(s_const, 11)
            pool.affine_select(out=ident[:, :], in_=ident[:, :], pattern=[[-1, P]], compare_op=ALU.not_equal,
                               fill=1.0, base=0, channel_multiplier=1).then_inc(s_const, 1)
            pool.affine_select(out=before[:, :], in_=ones_b[:, :], pattern=[[1, P]], compare_op=ALU.is_ge,
                               fill=0.0, base=-1, channel_multiplier=-1).then_inc(s_const, 1)
            pool.wait_ge(s_empty, 1 + 16 * N_EMPTY)
            def scatter(g):
                for s in range(SUBS):
                    pool.wait_ge(s_at, g * 2 * SUBS + 2 * s + 2)
                    pool.sem_inc(s_passed, 1)
                    for c in range(LOT):
                        pool.indirect_dma_start(
                            out=records, out_offset=bass.IndirectOffsetOnAxis(ap=pos_at[0:EP, s, c:c + 1], axis=0),
                            in_=rec_out[0:EP, s, 4 * c:4 * c + 4], in_offset=None, compute_op=ALU.bypass).then_inc(s_scat[s], 16)
            loop(pool, GROUPS, scatter)
            pool.wait_ge(s_start, 1)

            def step(i, k):
                def tile(off, j):
                    return i * RING + (k + off) * SB + j

                if live(i, k, 2):
                    o = (k + 2) % SPB * SB
                    if live(i, k, -2):
                        pool.wait_ge(s_tmax, i * SPB + k - 1)
                    pool.tensor_copy(rec[:, o:o + SB, :], rec_words[:, bass.ds(tile(2, 0), SB), :]).then_inc(s_rec, 1)
                if live(i, k, -2):
                    pool.wait_ge(s_shift, i * SPB + (k - 1))
                    pool.sem_inc(s_passed, 1)
                    pool.tensor_copy(shift_all[:, bass.ds(i * SPB + (k - 2), 1), :].rearrange("p a h -> p (a h)"),
                                     shift[:, (k - 2) % SPB, :]).then_inc(s_shift_all, 1)
                if live(i, k, 1):
                    pool.wait_ge(s_rec, i * SPB + k + 2)
                    for j in range(SB):
                        slot = ((k + 1) * SB + j) % RING
                        if live(i, k, -3):
                            pool.wait_ge(s_agg, tile(-3, j) + 1)
                        pool.sem_inc(s_passed, 1)
                        pool.memset(z_t[:, slot, ZW:QW], 0.0).then_inc(s_z_zero, 1)
                        pool.wait_ge(s_z_zero, tile(1, j) + 1)
                        pool.wait_ge(s_z_ev, tile(1, j) + 1)
                        pool.sem_inc(s_passed, 1)
                        pool.indirect_dma_start(
                            out=z_t[:, slot, :], out_offset=None, in_=qf_table,
                            in_offset=bass.IndirectOffsetOnAxis(ap=rec[:, slot, 3:4].bitcast(I32), axis=0),
                            compute_op=ALU.add).then_inc(s_gather[slot], 16)

            pipeline(pool, step)

        @block.tensor
        def _(pe):
            pe.wait_ge(s_const, 13)
            pe.matmul(psum[:, 0, 0:CH * W], zeros_b, iota_win[:, :, :].rearrange("p c w -> p (c w)"), start=True, stop=False,
                      skip_group_check=True).then_inc(s_hist, 1)
            def count_windows(g):
                for q in range(CPI // CH):
                    pe.wait_ge(s_hist_oh, g * (CPI // CH) + q + 1)
                    pe.matmul(psum[:, 0, 0:CH * W], ones_b[0:EP, :], win_oh[0:EP, q % 2, :, :].rearrange("p c w -> p (c w)"),
                              start=False, stop=False, skip_group_check=True).then_inc(s_hist, 1)
            loop(pe, GROUPS, count_windows)
            pe.wait_ge(s_base, 4)
            pe.matmul(psum[0:W, 1, 0:1], ends[0:1, :], ones_f[0:1, 0:1], start=True, stop=True).then_inc(s_tab_mm, 1)
            pe.wait_ge(s_base, 6)
            for n, o in enumerate(range(0, NT, 512)):
                m = min(512, NT - o)
                pe.matmul(psum[0:1, 2 + n, 0:m], ones_b[0:W, 0:1], win_done[0:W, o:o + m], start=True, stop=True).then_inc(s_tab_mm, 1)
            pe.wait_ge(s_weights, N_W)
            pe.wait_ge(s_base, 6 + N_TAB)
            pe.sem_inc(s_count, 1)

            def prefix(g, q):
                n = g * (CPI // CH) + q
                pe.wait_ge(s_oh, n + 1)
                since(pe, s_carry, n)
                o = psum[:, q % 2, :]
                for c in range(CH):
                    oh = win_oh[0:EP, q % 2, c, :]
                    pe.matmul(o[:, (c + 1) * W:(CH + 1) * W].rearrange("p (c w) -> p c w", w=W), ones_b[0:EP, :],
                              oh.unsqueeze(1).to_broadcast([EP, CH - c, W]), start=(c == 0), stop=False, skip_group_check=True)
                    mm = pe.matmul(o[:, c * W:(c + 1) * W], before[0:EP, :], oh, start=False, stop=(c == CH - 1),
                                   skip_group_check=True)
                mm.then_inc(s_count, 1)

            def hidden(g, m):
                since(pe, s_h_ev, g * MC + max(m - 1, 0))
                if m == 0:
                    pe.wait_ge(s_xt, g * KC + KC)
                    since(pe, s_q_ev, g * 4)
                h, c = m // (HID // P), m % (HID // P)
                for k in range(KC):
                    mm = pe.matmul(psum[:, 2 + m % 2, 0:NG], w1_s[:, k, h, c * P:(c + 1) * P], x_t[:, k, :],
                                   start=(k == 0), stop=(k == KC - 1))
                mm.then_inc(s_h_mm, 1)

            def feats(g, q):
                if q:
                    pe.wait_ge(s_f_ev, g * 2 + 1)
                for m in range(MC // 2 * q, MC // 2 * (q + 1)):
                    pe.wait_ge(s_h_ev, g * MC + m + 1)
                    mm = pe.matmul(psum[:, 4, 0:NG], w2_s[:, m, :], h_t[:, m, :], start=(m == MC // 2 * q),
                                   stop=(m == MC // 2 * (q + 1) - 1))
                mm.then_inc(s_f_mm, 1)

            def window(g, w):
                n = g * 4 + w
                at = slice(w * WN, (w + 1) * WN)
                if w == 0:
                    pe.wait_ge(s_f_ev, g * 2 + 2)
                    pe.wait_ge(s_h_ev, g * MC + MC)
                since(pe, s_p_ev, n)
                for q in range(2):
                    mm = pe.matmul(psum[0:WN, 5 + q, 0:HALF], f_t[:, q, at], ad_s[:, q, 0, :], start=True, stop=True)
                mm.then_inc(s_p_mm, 1)
                since(pe, s_t_ev, n)
                for q in range(2):
                    mm = pe.transpose(psum[0:WN, 7, q * P:(q + 1) * P], f_t[:, q, at], ident[:, :])
                mm.then_inc(s_t_mm, 1)
                since(pe, s_q_ev, n)
                for q in range(2):
                    mm = pe.matmul(psum[0:WN, 2 + q, 0:HALF], f_t[:, q, at], ad_s[:, q, 1, :], start=True, stop=True)
                mm.then_inc(s_q_mm, 1)

            beside = {0: [], 1: [(hidden, 0)], 2: [(hidden, 1), (hidden, 2)], 3: [(hidden, 3)], 4: [(hidden, 4), (hidden, 5)],
                      5: [(hidden, 6)], 6: [(hidden, 7)], 7: [(feats, 0)], 8: [(feats, 1)],
                      9: [(window, 0)], 11: [(window, 1)], 13: [(window, 2)], 15: [(window, 3)]}
            assert MC == 8 and CPI // CH == 16

            def group(g):
                pe.wait_ge(s_x, g * 16 + 16)
                since(pe, s_t_ev, g * 4)
                since(pe, s_f_ev, g * 2)
                for c in range(KC):
                    for w in range(4):
                        mm = pe.transpose(psum[:, [7, 4][c], w * WN:(w + 1) * WN], x_rows[0:WN, w, c * P:(c + 1) * P],
                                          ident[0:WN, 0:WN])
                mm.then_inc(s_xt_mm, 1)
                for q in range(CPI // CH):
                    prefix(g, q)
                    for product, n in beside.get(q, []):
                        product(g, n)
            loop(pe, GROUPS, group)
            pe.wait_ge(s_start, 1)
            pe.sem_inc(s_z_mm, 1)

            def z_parts(t, slot, w):
                pe.wait_ge(s_win_ready, w + 1)
                for half in range(2):
                    for part in range(3):
                        mm = pe.matmul(psum[:, slot % 2 * 2 + half, 0:HALF], onehot_t[:, slot % (RING // 2), :],
                                       p_flat[:, bass.ds((w % 2) * (3 * ZW) + (part * ZW + half * HALF), HALF)],
                                       start=(part == 0), stop=(part == 2))
                mm.then_inc(s_z_mm, 1)

            def sum_up(i, k, off, j):
                if live(i, k, off):
                    t, slot = i * RING + (k + off) * SB + j, ((k + off) * SB + j) % RING
                    pe.wait_ge(s_wf, t + 1)
                    since(pe, s_acc, t - 1)
                    pe.matmul(psum[:, 4 + slot % 2, 0:H * HF], onehot[:, slot, :], z_t[:, slot, ZW:QW], start=True, stop=True)\
                      .then_inc(s_agg, 1)

            def step(i, k):
                def tile(off, j):
                    return i * RING + (k + off) * SB + j

                if live(i, k, 1):
                    pack = pe.value_load(win_pack[0:1, bass.ds(i * SPB + (k + 1), 1)], min_val=0, max_val=(1 << 28) - 1)
                sum_up(i, k, -2, 1)
                for j in range(SB):
                    if j == SB - 1 and live(i, k, 2):
                        pe.wait_ge(s_onehot, i * SPB + k + 3)
                        if live(i, k, 1):
                            pe.wait_ge(s_oht, i * SPB + k + 2)
                        for v in range(SB):
                            mm = pe.transpose(psum[:, 6, v * P:(v + 1) * P], onehot[:, ((k + 2) * SB + v) % RING, :], ident[:, :])
                        mm.then_inc(s_oht_mm, 1)
                    if live(i, k, 1):
                        w = win_at(pack, j)
                        slot = ((k + 1) * SB + j) % RING
                        if j == 0:
                            pe.wait_ge(s_oht, i * SPB + k + 2)
                        since(pe, s_z_ev, tile(1, j) - 1)
                        z_parts(tile(1, j), slot, w)
                    if j == 0 and live(i, k, -1):
                        pe.wait_ge(s_tmax, i * SPB + k)
                        pe.transpose(psum[0:H, 7, 0:P], tile_max[:, (k - 1) % SPB, :], ident[:, :]).then_inc(s_tmax_t, 1)
                    if j == 1 and live(i, k, -1):
                        pe.wait_ge(s_diag, i * SPB + k)
                        pe.matmul(psum[:, 7, P:P + H], ones_f[0:H, :], max_diag[:, (k - 1) % SPB, :], start=True, stop=True)\
                          .then_inc(s_max_b, 1)
                    if j < SB - 1:
                        sum_up(i, k, *WEIGHTED[j])

            pipeline(pe, step)

        @block.scalar
        def _(act):
            act.wait_ge(s_weights, N_W)
            def group(g):
                act.wait_ge(s_xt_mm, g + 1)
                since(act, s_h_mm, g * MC)
                for c in range(KC):
                    act.activation(x_t[:, c, :], psum[:, [7, 4][c], 0:NG], ACT.Copy).then_inc(s_xt, 1)
                since(act, s_f_mm, g * 2)
                for m in range(MC):
                    act.wait_ge(s_h_mm, g * MC + m + 1)
                    act.activation(h_t[:, m, :], psum[:, 2 + m % 2, 0:NG], ACT.Relu, bias=b1_s[:, m:m + 1]).then_inc(s_h_ev, 1)
                since(act, s_q_mm, g * 4)
                for q in range(2):
                    act.wait_ge(s_f_mm, g * 2 + q + 1)
                    act.activation(f_t[:, q, :], psum[:, 4, 0:NG], ACT.Identity, bias=b2_s[:, q:q + 1]).then_inc(s_f_ev, 1)
                for w in range(4):
                    n = g * 4 + w
                    act.wait_ge(s_p_ev, n + 1)
                    since(act, s_p_st[w % 2], g * 32 + w // 2 * 16)
                    act.activation(p_out[0:WN, w % 2, 0:ZW], p_f[0:WN, :], ACT.Copy).then_inc(s_p_hi, 1)
                    act.wait_ge(s_q_mm, n + 1)
                    since(act, s_qf_st[w % 2], g * 32 + w // 2 * 16)
                    act.activation(qf_out[0:WN, w % 2, 0:ZW].rearrange("p (q n) -> p q n", q=2), psum[0:WN, 2:4, 0:HALF],
                                   ACT.Copy).then_inc(s_q_ev, 1)
                    act.wait_ge(s_p_rest, n + 1)
                    act.activation(p_out[0:WN, w % 2, ZW:2 * ZW], p_f[0:WN, :], ACT.Copy).then_inc(s_p_mid, 1)
            loop(act, GROUPS, group)
            act.wait_ge(s_start, 1)

            def weighted(i, k, off, j):
                if live(i, k, off):
                    slot = ((k + off) * SB + j) % RING
                    act.wait_ge(s_w, i * SPB + (k + off) + 1)
                    for h in range(H):
                        o = ZW + h * HF
                        op = act.activation(z_t[:, slot, o:o + DO], z_t[:, slot, o:o + DO], ACT.Copy, scale=z_t[:, slot, o + DO:o + HF])
                    op.then_inc(s_wf, 1)

            def step(i, k):
                def tile(off, j):
                    return i * RING + (k + off) * SB + j

                for j in range(SB):
                    if j == 2 and live(i, k, -1):
                        o, kk = (k - 1) % SPB * SB, (k - 1) % SPB
                        act.wait_ge(s_esh, i * SPB + k)
                        act.activation(z_t[:, o:o + SB, ZW:QW].rearrange("p t (h f) -> p t h f", f=HF)[:, :, :, DO],
                                       e_sh[:, o:o + SB, :], ACT.Exp).then_inc(s_w, 1)
                        act.wait_ge(s_drop, i * SPB + k)
                        act.activation(decay[:, kk, :], drop[:, kk, :], ACT.Exp).then_inc(s_decay, 1)
                    weighted(i, k, *WEIGHTED[j])
                    if j == SB - 1 and live(i, k, 2):
                        o = k % 2 * SB
                        act.wait_ge(s_oht_mm, i * SPB + k + 3)
                        if live(i, k, 0):
                            act.wait_ge(s_z_mm, tile(0, SB - 1) + 2)
                        act.activation(onehot_t[:, o:o + SB, :].rearrange("p t n -> p (t n)"), psum[:, 6, :], ACT.Copy).then_inc(s_oht, 1)
                    if live(i, k, 1):
                        slot = ((k + 1) * SB + j) % RING
                        act.wait_ge(s_z_mm, tile(1, j) + 2)
                        if live(i, k, -3):
                            act.wait_ge(s_agg, tile(-3, j) + 1)
                        act.activation(z_t[:, slot, 0:ZW].rearrange("p (q n) -> p q n", q=2),
                                       psum[:, slot % 2 * 2:slot % 2 * 2 + 2, 0:HALF], ACT.Copy).then_inc(s_z_ev, 1)

            pipeline(act, step)
            with act.Fori(0, W // CG) as g:
                act.wait_ge(s_c, g * C_STEPS + CG)
                act.activation(c_s[0:WN], c_e[0:WN], ACT.Exp).then_inc(s_c_exp, 1)
                act.wait_ge(s_c, g * C_STEPS + C_VAR)
                act.activation(c_sd[0:WN, :], c_mv[0:WN, :, 1], ACT.Sqrt, bias=c_eps[0:WN, :]).then_inc(s_c_std, 1)

        @block.vector
        def _(dve):
            R = rec_src[0:EP, :].rearrange("p (c n) -> p c n", n=4)
            RB = rec_src[0:EP, :].bitcast(BF16).rearrange("p (c n) -> p c n", n=8)
            R0, R1, R2 = (R[:, :, n] for n in range(3))
            R1I = R[:, :, 1:2].bitcast(I32)[:, :, 0]
            ta = tmp_a[0:EP, :]
            wt = weight_f[0:EP, :]
            dve.wait_ge(s_edges, 48)
            edge_steps = [
                lambda: dve.tensor_copy(ta, src_i[0:EP, :]),
                lambda: dve.tensor_scalar(R1I, ta, 1.0 / WN, None, ALU.mult),
                lambda: dve.tensor_copy(R2, R1I),
                lambda: dve.scalar_tensor_tensor(out=R0, in0=R2, scalar=-float(WN), in1=ta, op0=ALU.mult, op1=ALU.add),
                lambda: dve.tensor_scalar(R1, R0, 0.0, None, ALU.is_lt),
                lambda: dve.tensor_tensor(edge_win[0:EP, :], R2, R1, ALU.subtract),
                lambda: dve.scalar_tensor_tensor(out=R0, in0=R1, scalar=float(WN), in1=R0, op0=ALU.mult, op1=ALU.add),
                lambda: dve.tensor_scalar(R0, R0, 1.0, None, ALU.add),
                lambda: dve.tensor_copy(RB[:, :, 2], wt),
                lambda: dve.tensor_tensor(ta, wt, RB[:, :, 2], ALU.subtract),
                lambda: dve.tensor_copy(RB[:, :, 3], ta),
                lambda: dve.tensor_tensor(ta, ta, RB[:, :, 3], ALU.subtract),
                lambda: dve.tensor_copy(RB[:, :, 4], ta),
                lambda: dve.memset(RB[:, :, 5], 0.0),
                lambda: dve.tensor_copy(R[:, :, 3:4].bitcast(I32)[:, :, 0], dst_i[0:EP, :]),
            ]
            for n, op in enumerate(edge_steps):
                if n:
                    dve.wait_ge(s_edge_step, n)
                op().then_inc(s_edge_step, 1)
            dve.wait_ge(s_const, 13)
            dve.wait_ge(s_edge_step, len(edge_steps))

            def edge_onehot(g, c, b):
                return dve.tensor_tensor(win_oh[0:EP, b, :, :],
                                         edge_win[0:EP, bass.ds(g * CPI + c, CH)].unsqueeze(2).to_broadcast([EP, CH, W]),
                                         iota_win[0:EP, :, :], ALU.is_equal)

            def count_windows(g):
                for q in range(CPI // CH):
                    since(dve, s_hist, g * (CPI // CH) + q)
                    edge_onehot(g, q * CH, q % 2).then_inc(s_hist_oh, 1)
            loop(dve, GROUPS, count_windows)
            dve.wait_ge(s_hist, EC // CH + 1)
            dve.tensor_reduce(counts[:, :], psum[:, 0, 0:CH * W].rearrange("p (c w) -> p w c", c=CH), AX_X, ALU.add).then_inc(s_base, 1)
            dve.wait_ge(s_base, 1)
            dve.tensor_scalar(sizes_i[:, :], counts[:, :], float(P - 1), None, ALU.add).then_inc(s_base, 1)
            dve.wait_ge(s_base, 2)
            dve.tensor_scalar(sizes_i[:, :], sizes_i[:, :], -P, None, ALU.bitwise_and).then_inc(s_base, 1)
            dve.wait_ge(s_base, 3)
            dve.tensor_copy(sizes[:, :], sizes_i[:, :]).then_inc(s_tab_step, 1)
            dve.wait_ge(s_tab_step, 1)
            dve.tensor_tensor_scan(ends[:, :], ones_f[:, 0:W], sizes[:, :], 0.0, ALU.mult, ALU.add).then_inc(s_base, 1)
            dve.wait_ge(s_base, 4)
            dve.tensor_tensor(count_t[:, 1, CH * W:(CH + 1) * W], ends[:, :], sizes[:, :], ALU.subtract).then_inc(s_tab_step, 1)
            dve.wait_ge(s_tab_mm, 1)
            dve.tensor_copy(end_col[0:W, :], psum[0:W, 1, 0:1]).then_inc(s_base, 1)
            dve.wait_ge(s_base, 5)
            dve.tensor_scalar(win_done[0:W, :], win_iota[0:W, :], end_col[0:W, :], None, ALU.is_ge).then_inc(s_base, 1)
            for n, o in enumerate(range(0, NT, 512)):
                m = min(512, NT - o)
                dve.wait_ge(s_tab_mm, n + 2)
                dve.tensor_scalar(win_of[:, o:o + m], psum[0:1, 2 + n, 0:m], float(W - 1), None, ALU.min).then_inc(s_base, 1)
            dve.wait_ge(s_base, 6 + N_TAB)
            quarter = win_of[:, :].rearrange("p (s j) -> p j s", j=SB)
            table_steps = [
                lambda: dve.tensor_copy(win_pack[:, :], quarter[:, 0, :]),
                lambda: dve.tensor_scalar(row_tmp[:, 0:NSB], quarter[:, 1, :], 7, None, ALU.logical_shift_left),
                lambda: dve.tensor_tensor(win_pack[:, :], win_pack[:, :], row_tmp[:, 0:NSB], ALU.bitwise_or),
                lambda: dve.tensor_scalar(row_tmp[:, 0:NSB], quarter[:, 2, :], 14, None, ALU.logical_shift_left),
                lambda: dve.tensor_tensor(win_pack[:, :], win_pack[:, :], row_tmp[:, 0:NSB], ALU.bitwise_or),
                lambda: dve.tensor_scalar(row_tmp[:, 0:NSB], quarter[:, 3, :], 21, None, ALU.logical_shift_left),
                lambda: dve.tensor_tensor(win_pack[:, :], win_pack[:, :], row_tmp[:, 0:NSB], ALU.bitwise_or),
                lambda: dve.memset(end_prev[:, :], 1),
                lambda: dve.tensor_scalar(end_prev[:, 2:W], ends[0:1, 0:W - 2], 1.0 / P, 1.0, ALU.mult, ALU.add),
                lambda: dve.tensor_scalar(sizes[0:1, :], ends[0:1, :], 1.0 / P, -1.0, ALU.mult, ALU.add),
                lambda: dve.tensor_scalar(last_sb[:, :], sizes[0:1, :], 0.0, None, ALU.max),
                lambda: dve.tensor_scalar(last_sb[:, :], last_sb[:, :], 2, None, ALU.logical_shift_right),
                lambda: dve.memset(last_sb[:, W - 1:W], NSB - 1),
            ]
            for n, op in enumerate(table_steps):
                dve.wait_ge(s_tab_step, n + 2)
                op().then_inc(s_tab_step, 1)
            dve.wait_ge(s_tab_step, len(table_steps) + 2)
            dve.wait_ge(s_weights, N_W)
            ar, rest, ap3 = a_row[0:1, :], a_rest[0:1, :], a_parts[0:1, :].rearrange("p (u n) -> p u n", u=3)
            dve.tensor_copy(ap3[:, 0, :], ar).then_inc(s_a_step, 1)
            dve.wait_ge(s_a_step, 1)
            dve.tensor_tensor(rest, ar, ap3[:, 0, :], ALU.subtract).then_inc(s_a_step, 1)
            dve.wait_ge(s_a_step, 2)
            dve.tensor_copy(ap3[:, 1, :], rest).then_inc(s_a_step, 1)
            dve.wait_ge(s_a_step, 3)
            dve.tensor_tensor(rest, rest, ap3[:, 1, :], ALU.subtract).then_inc(s_a_step, 1)
            dve.wait_ge(s_a_step, 4)
            dve.tensor_copy(ap3[:, 2, :], rest).then_inc(s_a_step, 1)

            dve.sem_inc(s_carry, 1)

            def picked(g, s, q):
                n = s * CHUNKS + q
                return g * (SUBS * (CHUNKS + 3)) + (n + 1 + n // CHUNKS * 3)

            def sort_onehot(g, s, q):
                n = g * (CPI // CH) + s * CHUNKS + q
                since(dve, s_count, n)
                since(dve, s_pos, picked(g, s, q - 2))
                edge_onehot(g, s * LOT + q * CH, q % 2).then_inc(s_oh, 1)

            def sort_pick(g, s, q):
                n = g * (CPI // CH) + s * CHUNKS + q
                dve.wait_ge(s_count, n + 2)
                dve.wait_ge(s_carry, n + 1)
                since(dve, s_pos, picked(g, s, q - 2))
                dve.tensor_tensor(count_t[:, q % 2, :].rearrange("p (c w) -> p c w", w=W),
                                  psum[:, q % 2, 0:(CH + 1) * W].rearrange("p (c w) -> p c w", w=W),
                                  count_t[:, (q + 1) % 2, CH * W:].unsqueeze(1).to_broadcast([P, CH + 1, W]), ALU.add).then_inc(s_carry, 1)
                dve.wait_ge(s_carry, n + 2)
                for c in range(CH):
                    own = count_t[0:EP, q % 2, c * W:(c + 1) * W]
                    op = dve.scalar_tensor_tensor(out=own, in0=own, scalar=1.0,
                                                  in1=win_oh[0:EP, q % 2, c, :], op0=ALU.mult, op1=ALU.mult,
                                                  accum_out=pos_f[0:EP, s, q * CH + c:q * CH + c + 1])
                op.then_inc(s_pos, 1)

            def sort_places(g, s):
                n = picked(g, s, CHUNKS - 1)
                dve.wait_ge(s_pos, n)
                since(dve, s_at, (g * SUBS + s) * 2)
                dve.tensor_copy(pos_i[0:EP, s, :], pos_f[0:EP, s, :]).then_inc(s_pos, 1)
                dve.wait_ge(s_pos, n + 1)
                dve.tensor_scalar(pos_p[0:EP, :], pos_i[0:EP, s, :], P - 1, None, ALU.bitwise_and).then_inc(s_pos, 1)
                dve.tensor_scalar(pos_t[0:EP, :], pos_i[0:EP, s, :], 7, None, ALU.logical_shift_right).then_inc(s_pos, 1)
                dve.wait_ge(s_pos, n + 3)
                since(dve, s_scat[s], g * (16 * LOT))
                dve.scalar_tensor_tensor(out=pos_at[0:EP, s, :], in0=pos_p[0:EP, :], scalar=float(NT), in1=pos_t[0:EP, :],
                                         op0=ALU.mult, op1=ALU.add).then_inc(s_at, 1)
                dve.tensor_copy(rec_out[0:EP, s, :].bitcast(I32),
                                rec_src[0:EP, bass.ds((g * CPI + s * LOT) * 4, LOT * 4)].bitcast(I32)).then_inc(s_at, 1)

            pf = p_f[0:WN, :]

            def p_sum(g, w):
                n, b = g * 4 + w, w % 2
                dve.wait_ge(s_p_mm, n + 1)
                since(dve, s_p_lo, n)
                dve.tensor_tensor(pf.rearrange("p (q n) -> p q n", q=2), psum[0:WN, 5:7, 0:HALF],
                                  ab1_b[0:WN, :].rearrange("p (q n) -> p q n", q=2), ALU.add).then_inc(s_p_ev, 1)
                dve.wait_ge(s_t_mm, n + 1)
                since(dve, s_qf_st[b], g * 32 + w // 2 * 16)
                dve.tensor_copy(qf_out[0:WN, b, ZW:QW].rearrange("p (h f) -> p h f", f=HF)[:, :, 0:DO],
                                psum[0:WN, 7, 0:H * DO].rearrange("p (h f) -> p h f", h=H)).then_inc(s_t_ev, 1)

            def p_rest(g, w):
                n, b = g * 4 + w, w % 2
                dve.wait_ge(s_p_hi, n + 1)
                dve.tensor_tensor(pf, pf, p_out[0:WN, b, 0:ZW], ALU.subtract).then_inc(s_p_rest, 1)

            def p_last(g, w):
                n, b = g * 4 + w, w % 2
                dve.wait_ge(s_p_mid, n + 1)
                dve.wait_ge(s_p_rest, n + 1)
                dve.tensor_tensor(p_out[0:WN, b, 2 * ZW:3 * ZW], pf, p_out[0:WN, b, ZW:2 * ZW], ALU.subtract).then_inc(s_p_lo, 1)

            beside = {10: [(p_sum, 0)], 11: [(p_rest, 0)], 12: [(p_last, 0), (p_sum, 1)], 13: [(p_rest, 1)],
                      14: [(p_last, 1), (p_sum, 2)], 15: [(p_rest, 2), (p_last, 2), (p_sum, 3), (p_rest, 3), (p_last, 3)]}

            def group(g):
                for n in range(SUBS * CHUNKS + 1):
                    if n < SUBS * CHUNKS:
                        sort_onehot(g, n // CHUNKS, n % CHUNKS)
                    if n:
                        sort_pick(g, (n - 1) // CHUNKS, (n - 1) % CHUNKS)
                        if n % CHUNKS == 0:
                            sort_places(g, (n - 1) // CHUNKS)
                        for work, w in beside.get(n - 1, []):
                            work(g, w)
            loop(dve, GROUPS, group)

            dve.wait_ge(s_start, 1)
            dve.memset(acc[:, :], 0.0).then_inc(s_acc_zero, 1)
            dve.memset(shift[:, SPB - 1, :], LOW).then_inc(s_acc_zero, 1)
            dve.wait_ge(s_acc_zero, 2)
            rec_b = rec[:, :, :].bitcast(BF16)

            def step(i, k):
                def tile(off, j):
                    return i * RING + (k + off) * SB + j

                def sbn(off):
                    return i * SPB + (k + off)

                if live(i, k, -2):
                    pack = dve.value_load(win_pack[0:1, bass.ds(sbn(-2), 1)], min_val=0, max_val=(1 << 28) - 1)
                kk, kp, o = (k - 1) % SPB, (k - 2) % SPB, (k - 1) % SPB * SB
                ev, er = e_val[:, o:o + SB, :], e_raw[:, o:o + SB, :]

                def bias():
                    dve.wait_ge(s_dot, tile(-1, SB - 1) + 1)
                    dve.tensor_tensor(ev, er, ab2_b[:, :].unsqueeze(1).to_broadcast([P, SB, H]), ALU.add).then_inc(s_e_bias, 1)

                def leaky():
                    dve.wait_ge(s_e_bias, sbn(0))
                    dve.scalar_tensor_tensor(out=er, in0=ev, scalar=0.2, in1=ev, op0=ALU.mult, op1=ALU.max).then_inc(s_e_leaky, 1)

                def mask():
                    dve.wait_ge(s_e_leaky, sbn(0))
                    dve.tensor_tensor(ev, er, rec_b[:, o:o + SB, 5:6].to_broadcast([P, SB, H]), ALU.add).then_inc(s_e_mask, 1)

                def tiles_max():
                    dve.wait_ge(s_e_mask, sbn(0))
                    dve.tensor_reduce(tile_max[:, kk, :], ev.rearrange("p t h -> p h t"), AX_X, ALU.max).then_inc(s_tmax, 1)

                def heads_max():
                    dve.wait_ge(s_tmax_t, sbn(0))
                    dve.tensor_reduce(head_max[:, kk:kk + 1], psum[0:H, 7, 0:P], AX_X, ALU.max).then_inc(s_head_max, 1)

                def diagonal():
                    dve.wait_ge(s_head_max, sbn(0))
                    dve.tensor_scalar(max_diag[:, kk, :], ident[0:H, 0:H], head_max[:, kk:kk + 1], None, ALU.mult).then_inc(s_diag, 1)

                def new_shift():
                    dve.wait_ge(s_max_b, sbn(0))
                    since(dve, s_shift, sbn(-1))
                    dve.tensor_tensor(shift[:, kk, :], psum[:, 7, P:P + H], shift[:, kp, :], ALU.max).then_inc(s_shift, 1)

                def shifted():
                    dve.wait_ge(s_shift, sbn(0))
                    dve.tensor_tensor(e_sh[:, o:o + SB, :], ev,
                                      shift[:, kk, :].unsqueeze(1).to_broadcast([P, SB, H]), ALU.subtract).then_inc(s_esh, 1)
                    dve.tensor_tensor(drop[:, kk, :], shift[:, kp, :], shift[:, kk, :], ALU.subtract).then_inc(s_drop, 1)

                def add_sums(j):
                    t = tile(-2, j)
                    a = acc[0:WN, bass.ds(win_at(pack, j) * (H * HF), H * HF)]
                    dve.wait_ge(s_decayed, sbn(-1)) if j == 0 else dve.wait_ge(s_acc, t)
                    dve.wait_ge(s_agg, t + 1)
                    dve.tensor_tensor(a, a, psum[0:WN, 4 + j % 2, 0:H * HF], ALU.add).then_inc(s_acc, 1)

                def decay_sums():
                    a = acc[0:WN, bass.ds(win_at(pack, 0) * (H * HF), H * HF)].rearrange("p (h f) -> p h f", h=H)
                    dve.wait_ge(s_decay, sbn(-1))
                    since(dve, s_acc, tile(-2, 0))
                    dve.tensor_tensor(a, a, decay[0:WN, (k - 2) % SPB, :].unsqueeze(2).to_broadcast([WN, H, HF]), ALU.mult)\
                       .then_inc(s_decayed, 1)

                def onehots():
                    oo = (k + 2) % SPB * SB
                    dve.wait_ge(s_rec, sbn(2) + 1)
                    if live(i, k, -2):
                        dve.wait_ge(s_agg, tile(-2, SB - 1) + 1)
                    dve.tensor_tensor(onehot[:, oo:oo + SB, 0:WN], iota_row[:, :].unsqueeze(1).to_broadcast([P, SB, WN]),
                                      rec[:, oo:oo + SB, 0:1].to_broadcast([P, SB, WN]), ALU.is_equal)
                    dve.tensor_copy(onehot[:, oo:oo + SB, WN:P], rec_b[:, oo:oo + SB, 2:5]).then_inc(s_onehot, 1)

                after = [[[(-1, bias)], [(-1, leaky)], [(-1, mask)], [(-1, tiles_max), (-2, decay_sums)]],
                         [[(-2, lambda: add_sums(0)), (-1, heads_max)], [(-1, diagonal)], [(-2, lambda: add_sums(1))], [(-1, new_shift)]],
                         [[(-1, shifted)], [(-2, lambda: add_sums(2))], [], [(2, onehots)]],
                         [[], [(-2, lambda: add_sums(3))], [], []]]
                for j in range(SB):
                    for h in range(H):
                        if live(i, k, 0):
                            slot = k * SB + j
                            if h == 0:
                                dve.wait_ge(s_gather[slot], i * 16 + 16)
                            own = z_t[:, slot, h * AT:(h + 1) * AT]
                            op = dve.scalar_tensor_tensor(out=own, in0=own, scalar=0.0,
                                                          in1=a2_b[:, h * AT:(h + 1) * AT], op0=ALU.max, op1=ALU.mult,
                                                          accum_out=e_raw[:, slot, h:h + 1])
                            if h == H - 1:
                                op.then_inc(s_dot, 1)
                        for off, work in after[j][h]:
                            if live(i, k, off):
                                work()

            pipeline(dve, step)

            dve.wait_ge(s_acc, NT)
            dve.wait_ge(s_shift_all, NSB)
            dve.memset(c_eps, EPS).then_inc(s_acc_zero, 1)
            dve.wait_ge(s_acc_zero, 3)
            def finish(g):
                a4 = acc_w[0:WN, bass.ds(g * CG, CG), :].rearrange("p w (h f) -> p w h f", f=HF)
                n = g * C_STEPS
                since(dve, s_c_exp, g)
                for v in range(CG):
                    s = dve.value_load(last_sb[0:1, bass.ds(g * CG + v, 1)], min_val=0, max_val=NSB - 1)
                    dve.tensor_tensor(c_e[0:WN, v, :], shift_flat[0:WN, bass.ds(s * H, H)], shift_flat[0:WN, (NSB - 1) * H:NSB * H],
                                      ALU.subtract).then_inc(s_c, 1)
                dve.wait_ge(s_c_exp, g + 1)
                dve.tensor_tensor(c_d[0:WN], a4[:, :, :, DO], c_s[0:WN], ALU.mult).then_inc(s_c, 1)
                dve.wait_ge(s_c, n + CG + 1)
                dve.tensor_scalar(c_d[0:WN], c_d[0:WN], 1e-10, None, ALU.add).then_inc(s_c, 1)
                dve.wait_ge(s_c, n + CG + 2)
                dve.reciprocal(c_r[0:WN], c_d[0:WN]).then_inc(s_c, 1)
                dve.wait_ge(s_c, n + CG + 3)
                dve.tensor_tensor(c_k[0:WN], c_r[0:WN], c_s[0:WN], ALU.mult).then_inc(s_c, 1)
                dve.wait_ge(s_c, n + CG + 4)
                y4 = c_y[0:WN].rearrange("p w (h d) -> p w h d", h=H)
                dve.tensor_tensor(y4, a4[:, :, :, 0:DO], c_k[0:WN].unsqueeze(3).to_broadcast([WN, CG, H, DO]), ALU.mult).then_inc(s_c, 1)
                dve.wait_ge(s_c, n + CG + 5)
                dve.wait_ge(s_c_x, g * 16 + 16)
                dve.tensor_tensor(c_y[0:WN], c_y[0:WN], c_x[0:WN], ALU.add).then_inc(s_c_y, 1)
                dve.wait_ge(s_c_y, g + 1)
                for v in range(CG):
                    dve.bn_stats(c_st[0:WN, v, :], c_y[0:WN, v, :]).then_inc(s_c, 1)
                dve.wait_ge(s_c, n + 2 * CG + 5)
                dve.sem_inc(s_passed_c, 1)
                for v in range(CG):
                    dve.bn_aggr(c_mv[0:WN, v, :], c_st[0:WN, v, :]).then_inc(s_c, 1)
                dve.wait_ge(s_c_std, g + 1)
                dve.reciprocal(c_is[0:WN, :], c_sd[0:WN, :]).then_inc(s_c, 1)
                dve.wait_ge(s_c, n + 3 * CG + 6)
                since(dve, s_c_out, g * 16)
                for v in range(CG):
                    op = dve.tensor_scalar(c_o[0:WN, v, :], c_y[0:WN, v, :], c_mv[0:WN, v, 0:1], c_is[0:WN, v:v + 1],
                                           ALU.subtract, ALU.mult)
                op.then_inc(s_c_ready, 1)
            loop(dve, W // CG, finish)


_INS = ["x", "src", "dst", "edge_weight", "L0_gnn_W1", "L0_gnn_b1", "L0_gnn_W2", "L0_gnn_b2",
        "L0_gnn_A1", "L0_gnn_ab1", "L0_gnn_A2", "L0_gnn_ab2"]


def kernel(**inputs):
    import numpy as _np
    import concourse.bacc as _bacc
    from concourse import mybir as _mybir
    from concourse.bass_utils import run_bass_kernel_spmd as _run

    nc = _bacc.Bacc("TRN2", target_bir_lowering=False, num_devices=1)
    arrays, args = {}, []
    for name in _INS:
        a = _np.ascontiguousarray(inputs[name])
        arrays[f"in_{name}_dram"] = a
        args.append(nc.dram_tensor(f"in_{name}_dram", a.shape, _mybir.dt.from_np(a.dtype), kind="ExternalInput").ap())
    args.append(nc.dram_tensor("out_0_dram", arrays["in_x_dram"].shape, _mybir.dt.float32, kind="ExternalOutput").ap())
    gnn_layer(nc, *args)
    r = _run(nc, [arrays], core_ids=[0])
    return r.results[0]["out_0_dram"]
```

```python
from contextlib import ExitStack

import concourse.bass as bass
from concourse import mybir

ALU = mybir.AluOpType
ACT = mybir.ActivationFunctionType
F32 = mybir.dt.float32
I32 = mybir.dt.int32
BF16 = mybir.dt.bfloat16
AX_X = mybir.AxisListType.X


def gnn_layer(nc, x, src, dst, weight, W1, b1, W2, b2, A1, ab1, A2, ab2, out):
    N, D = x.shape
    E = src.shape[0]
    H, _, HID = W1.shape
    DO = W2.shape[2]
    AT = 2 * DO + 1
    P = 128
    WN = 125
    W = N // WN
    GROUPS = W // 4
    EP = 125
    EC = E // EP
    CPI = EC // GROUPS
    SUBS = 4
    LOT = CPI // SUBS
    CH = 4
    CHUNKS = LOT // CH
    assert N == WN * W and E == EP * EC and CPI * GROUPS == EC and CHUNKS * CH * SUBS == CPI
    ZW = H * AT
    HF = DO + 1
    QW = ZW + H * HF
    HALF = 2 * AT
    SB = 4
    RING = 16
    SPB = RING // SB
    NT = (E + W * (P - 1)) // P
    NT = -(-NT // RING) * RING
    NSB = NT // SB
    BODIES = NT // RING
    KC = D // P
    MC = H * HID // P
    NG = 4 * WN
    HI, LO = 16, 8
    HCOL = P // HI
    HB = 32
    assert HI <= W <= HI * LO and EC % (2 * HB) == 0
    EPS = 1e-5
    LOW = -1e30

    qf_table = nc.dram_tensor("qf_table", (N, QW), F32, kind="Internal").ap()
    p_table = nc.dram_tensor("p_table", (N, 3 * ZW), BF16, kind="Internal").ap()
    records = nc.dram_tensor("records", (P * NT, 4), F32, kind="Internal").ap()
    shift_rows = nc.dram_tensor("shift_rows", (NSB, H), F32, kind="Internal").ap()

    ctx = ExitStack()
    with ctx:
        def sb(name, shape, dt=F32):
            return ctx.enter_context(nc.sbuf_tensor(name, shape, dt))

        def sem(name):
            return ctx.enter_context(nc.semaphore(name))

        acc = sb("acc", [P, max(W * H * HF, 25600)])
        z = sb("z", [P, RING * QW])
        rec_all = sb("rec_all", [P, NT * 4])
        p_win = sb("p_win", [P, 2, 3 * ZW], BF16)
        ident = sb("ident", [P, P])
        ones_f = sb("ones_f", [P, P])
        ones_b = sb("ones_b", [P, P], BF16)
        before = sb("before", [P, P], BF16)
        iota_row = sb("iota_row", [P, WN])
        iota_win = sb("iota_win", [P, CH, W], BF16)
        a2_b = sb("a2_b", [P, ZW])
        ab2_b = sb("ab2_b", [P, H])
        onehot = sb("onehot", [P, RING, P])
        onehot_t = sb("onehot_t", [P, RING // 2, P], BF16)
        rec = sb("rec", [P, RING, 4])
        bias_mask = sb("bias_mask", [P, RING, H])
        e_raw = sb("e_raw", [P, RING, H])
        e_val = sb("e_val", [P, RING, H])
        tile_max = sb("tile_max", [P, SPB, H])
        head_max = sb("head_max", [H, SPB])
        max_diag = sb("max_diag", [H, SPB, H])
        shift = sb("shift", [P, SPB, H])
        e_sh = sb("e_sh", [P, RING, H])
        drop = sb("drop", [P, SPB, H])
        decay = sb("decay", [P, SPB, H])
        shift_all = sb("shift_all", [P, NSB, H])
        last_sb = sb("last_sb", [P, W], I32)
        end_prev = sb("end_prev", [1, W], I32)
        win_pack = sb("win_pack", [1, NSB], I32)
        psum = ctx.enter_context(nc.psum_tensor("psum", [P, 8, 512], F32))

        win_of = onehot[0:1, :, :].rearrange("p t n -> p (t n)").bitcast(I32)[:, 0:NT]
        row_tmp = onehot_t[0:1, :, :].rearrange("p t n -> p (t n)").bitcast(I32)[:, 0:NSB]
        assert NT <= RING * P
        used = [0]

        def carve(n):
            used[0] += n
            return acc[:, used[0] - n:used[0]]

        w1_s = carve(KC * H * HID).rearrange("p (k h n) -> p k h n", k=KC, h=H)
        w2_s = carve(MC * P).rearrange("p (m n) -> p m n", m=MC)
        ad_s = carve(2 * 2 * HALF).rearrange("p (q u n) -> p q u n", q=2, u=2)
        ab1_b = carve(ZW)
        b1_s = carve(MC)
        b2_s = carve(2)
        x_rows = carve(4 * D).rearrange("p (w n) -> p w n", w=4)
        x_t = carve(KC * NG).rearrange("p (k n) -> p k n", k=KC)
        h_t = carve(MC * NG).rearrange("p (m n) -> p m n", m=MC)
        f_t = carve(2 * NG).rearrange("p (q n) -> p q n", q=2)
        p_f = carve(ZW)
        p_out = carve(2 * 3 * ZW // 2).bitcast(BF16).rearrange("p (b n) -> p b n", b=2)
        qf_out = carve(2 * QW).rearrange("p (b n) -> p b n", b=2)
        assert used[0] <= 16000
        a_row = carve(ZW)
        a_rest = carve(ZW)
        a_parts = carve(3 * ZW // 2 + 2).bitcast(BF16)[:, 0:3 * ZW]
        src_i = carve(EC).bitcast(I32)
        dst_i = carve(EC).bitcast(I32)
        tmp_a = carve(EC)
        edge_hi = carve(EC // 2).bitcast(BF16)
        edge_lo = carve(EC // 2).bitcast(BF16)
        hi_oh = carve(2 * HB * HI // 2).bitcast(BF16).rearrange("p (b c n) -> p b c n", b=2, c=HB)
        lo_oh = carve(2 * HB * LO // 2).bitcast(BF16).rearrange("p (b c n) -> p b c n", b=2, c=HB)
        same_col = carve(HCOL * LO).rearrange("p (c n) -> p c n", c=HCOL)
        same_hi = carve(HI * LO).rearrange("p (h n) -> p h n", h=HI)
        by_col = carve(HCOL * LO).rearrange("p (c n) -> p c n", c=HCOL)
        by_lo = carve(LO)
        by_hi = carve(HI * LO).rearrange("p (h n) -> p h n", h=HI)
        assert used[0] <= 25600
        used_z = [0]

        def carve_z(n):
            used_z[0] += n
            return z[:, used_z[0] - n:used_z[0]]

        rec_src = carve_z(EC * 4)
        edge_win = carve_z(EC // 2).bitcast(BF16)
        win_oh = carve_z(2 * CH * W // 2).bitcast(BF16).rearrange("p (b c w) -> p b c w", b=2, c=CH)
        count_t = carve_z(2 * (CH + 1) * W).rearrange("p (b n) -> p b n", b=2)
        pos_f = carve_z(SUBS * LOT).rearrange("p (s n) -> p s n", s=SUBS)
        pos_i = carve_z(SUBS * LOT).bitcast(I32).rearrange("p (s n) -> p s n", s=SUBS)
        pos_p = carve_z(LOT).bitcast(I32)
        pos_t = carve_z(LOT).bitcast(I32)
        pos_at = carve_z(SUBS * LOT).bitcast(I32).rearrange("p (s n) -> p s n", s=SUBS)
        rec_out = carve_z(SUBS * LOT * 4).rearrange("p (s n) -> p s n", s=SUBS)
        win_iota = carve_z(NT)
        counts = carve_z(W)
        sizes_i = carve_z(W).bitcast(I32)
        sizes = carve_z(W)
        ends = carve_z(W)
        end_col = carve_z(1)
        zeros_b = carve_z(P // 2 + 1).bitcast(BF16)[:, 0:P]
        win_done = carve_z(NT // 2).bitcast(BF16)
        assert used_z[0] <= RING * QW
        weight_f = rec_all[:, 0:EC]
        empty = p_win[:, :, :].rearrange("p a n -> p (a n)").bitcast(F32)[:, 0:SB * 4 * 16]

        p_flat = p_win[:, :, :].rearrange("p a n -> p (a n)")
        shift_flat = shift_all[:, :, :].rearrange("p s h -> p (s h)")
        z_t = z[:, :].rearrange("p (t n) -> p t n", t=RING)
        acc_w = acc[:, 0:W * H * HF].rearrange("p (w n) -> p w n", w=W)
        rec_words = rec_all[:, :].rearrange("p (t n) -> p t n", n=4)

        s_const = sem("s_const")
        s_weights = sem("s_weights")
        s_edges = sem("s_edges")
        s_edge_step = sem("s_edge_step")
        s_a_step = sem("s_a_step")
        s_a_rows = sem("s_a_rows")
        s_empty = sem("s_empty")
        s_hist_oh = sem("s_hist_oh")
        s_hist = sem("s_hist")
        s_masks = sem("s_masks")
        s_parts = sem("s_parts")
        s_fold = sem("s_fold")
        s_fold_mm = sem("s_fold_mm")
        s_base = sem("s_base")
        s_tab_mm = sem("s_tab_mm")
        s_tab_step = sem("s_tab_step")
        s_acc_zero = sem("s_acc_zero")
        s_passed = sem("s_passed")
        s_passed_c = sem("s_passed_c")
        s_x = sem("s_x")
        s_xt_mm = sem("s_xt_mm")
        s_xt = sem("s_xt")
        s_h_mm = sem("s_h_mm")
        s_h_ev = sem("s_h_ev")
        s_f_mm = sem("s_f_mm")
        s_f_ev = sem("s_f_ev")
        s_p_mm = sem("s_p_mm")
        s_p_ev = sem("s_p_ev")
        s_p_hi = sem("s_p_hi")
        s_p_rest = sem("s_p_rest")
        s_p_mid = sem("s_p_mid")
        s_p_lo = sem("s_p_lo")
        s_t_mm = sem("s_t_mm")
        s_t_ev = sem("s_t_ev")
        s_q_mm = sem("s_q_mm")
        s_q_ev = sem("s_q_ev")
        s_p_st = [sem(f"s_p_st{n}") for n in range(2)]
        s_qf_st = [sem(f"s_qf_st{n}") for n in range(2)]
        s_oh = sem("s_oh")
        s_count = sem("s_count")
        s_carry = sem("s_carry")
        s_pos = sem("s_pos")
        s_at = sem("s_at")
        s_scat = [sem(f"s_scat{n}") for n in range(SUBS)]
        s_rec_first = sem("s_rec_first")
        s_rec_all = sem("s_rec_all")
        s_start = sem("s_start")
        s_win = [sem(f"s_win{n}") for n in range(2)]
        s_win_ready = sem("s_win_ready")
        s_rec = sem("s_rec")
        s_onehot = sem("s_onehot")
        s_oht_mm = sem("s_oht_mm")
        s_oht = sem("s_oht")
        s_z_mm = sem("s_z_mm")
        s_z_ev = sem("s_z_ev")
        s_z_zero = sem("s_z_zero")
        s_gather = [sem(f"s_gather{n}") for n in range(RING)]
        s_dot = sem("s_dot")
        s_e_bias = sem("s_e_bias")
        s_e_leaky = sem("s_e_leaky")
        s_bias_mask = sem("s_bias_mask")
        s_head_max = sem("s_head_max")
        s_drop = sem("s_drop")
        s_decay = sem("s_decay")
        s_decayed = sem("s_decayed")
        s_shift_all = sem("s_shift_all")
        s_tmax = sem("s_tmax")
        s_tmax_t = sem("s_tmax_t")
        s_diag = sem("s_diag")
        s_max_b = sem("s_max_b")
        s_shift = sem("s_shift")
        s_esh = sem("s_esh")
        s_w = sem("s_w")
        s_wf = sem("s_wf")
        s_wf_last = sem("s_wf_last")
        s_agg = sem("s_agg")
        s_acc = sem("s_acc")
        s_c_x = [sem(f"s_c_x{n}") for n in range(2)]
        s_c_shifts = sem("s_c_shifts")
        s_c_const = sem("s_c_const")
        s_c_last = sem("s_c_last")
        s_c_diff = sem("s_c_diff")
        s_c_exp = sem("s_c_exp")
        s_c_onehot = sem("s_c_onehot")
        s_c_pick = sem("s_c_pick")
        s_c_factor = sem("s_c_factor")
        s_c_coef = sem("s_c_coef")
        s_c_y = sem("s_c_y")
        s_c_add = sem("s_c_add")
        s_c_stats = sem("s_c_stats")
        s_c_var = sem("s_c_var")
        s_c_std = sem("s_c_std")
        s_c_inv = sem("s_c_inv")
        s_c_bias = sem("s_c_bias")
        s_c_ready = sem("s_c_ready")
        s_c_out = [sem(f"s_c_out{n}") for n in range(2)]

        CG = 5
        CGROUPS = W // CG
        CR = 4
        SC = next(NSB // n for n in range(1, NSB) if NSB % n == 0 and NSB // n <= P)
        KS = NSB // SC
        assert CGROUPS * CG == W and CGROUPS % CR == 0
        used_c = [0, 0]

        def carve_c(n, arena):
            used_c[arena] += n
            return (z, rec_all)[arena][:, used_c[arena] - n:used_c[arena]]

        c_x = carve_c(2 * CG * D, 0).rearrange("p (b w n) -> p b w n", b=2, w=CG)
        c_y = carve_c(CR * CG * D, 0).rearrange("p (b w n) -> p b w n", b=CR, w=CG)
        c_o = carve_c(2 * CG * D, 0).rearrange("p (b w n) -> p b w n", b=2, w=CG)
        assert used_c[0] <= RING * QW
        c_id = carve_c(KS, 1)
        c_last = carve_c(W, 1)
        c_shift = carve_c(KS * H, 1).rearrange("p (k h) -> p k h", k=KS)
        c_exp = carve_c(KS * H, 1).rearrange("p (k h) -> p k h", k=KS)
        c_oh = carve_c(KS * W, 1).rearrange("p (k w) -> p k w", k=KS)
        c_pick = carve_c(KS * W * H, 1).rearrange("p (k w h) -> p k w h", k=KS, w=W)
        c_s = carve_c(W * H, 1).rearrange("p (w h) -> p w h", w=W)
        c_d = carve_c(W * H, 1).rearrange("p (w h) -> p w h", w=W)
        c_k = carve_c(W * H, 1).rearrange("p (w h) -> p w h", w=W)
        c_st = carve_c(CR * CG * 6, 1).rearrange("p (b w n) -> p b w n", b=CR, w=CG)
        c_mv = carve_c(CR * CG * 2, 1).rearrange("p (b w n) -> p b w n", b=CR, w=CG)
        c_sd = carve_c(CR * CG, 1).rearrange("p (b w) -> p b w", b=CR)
        c_is = carve_c(CR * CG, 1).rearrange("p (b w) -> p b w", b=CR)
        c_nb = carve_c(CR * CG, 1).rearrange("p (b w) -> p b w", b=CR)
        c_eps = carve_c(1, 1)
        assert used_c[1] <= NT * 4

        block = ctx.enter_context(nc.Block())

        N_W = 16 * (KC + MC + 2 * H + 5 + 2)
        N_EDGE = 13
        N_PARTS = 7
        N_TAB_STEPS = 15
        N_EMPTY = -(-NT * 4 // (SB * 4 * 16))
        N_TAB = -(-NT // 512)

        def live(i, k, off):
            return not isinstance(i, int) or 0 <= i * SPB + k + off < NSB

        def since(eng, semaphore, count):
            if not (isinstance(count, int) and count <= 0):
                eng.wait_ge(semaphore, count)

        def loop(eng, n, body):
            body(0)
            with eng.Fori(1, n) as g:
                body(g)

        def group_at(g):
            return slice(g, g + 1) if isinstance(g, int) else bass.ds(g, 1)

        def live_c(i, k, off):
            return not isinstance(i, int) or 0 <= i * CR + k + off < CGROUPS

        def finish_pipeline(eng, step):
            for k in range(CR):
                step(0, k)
            with eng.Fori(1, CGROUPS // CR) as i:
                for k in range(CR):
                    step(i, k)
            step(CGROUPS // CR, 0)
            step(CGROUPS // CR, 1)

        def win_at(pack, j):
            return nc.s_assert_within((pack // (1 << 7 * j)) % 128 if j else pack % 128, 0, W - 1,
                                      skip_runtime_bounds_check_because="the table is clipped at W - 1")

        def pipeline(eng, step):
            step(-1, 2)
            step(-1, 3)
            for k in range(SPB):
                step(0, k)
            with eng.Fori(1, BODIES - 1) as i:
                for k in range(SPB):
                    step(i, k)
            for k in range(SPB):
                step(BODIES - 1, k)
            step(BODIES, 0)
            step(BODIES, 1)


        @block.sync
        def _(sp):
            sp.dma_start(src_i[0:EP, :], src.rearrange("(p c) -> p c", p=EP)).then_inc(s_edges, 16)
            sp.dma_start(weight_f[0:EP, :], weight.rearrange("(p c) -> p c", p=EP)).then_inc(s_edges, 16)
            sp.dma_start(dst_i[0:EP, :], dst.rearrange("(p c) -> p c", p=EP)).then_inc(s_edges, 16)
            for k in range(KC):
                sp.dma_start(w1_s[:, k, :, :], W1[:, k * P:(k + 1) * P, :].rearrange("h p n -> p h n")).then_inc(s_weights, 16)
            sp.wait_ge(s_const, 2)
            for m in range(MC):
                h, c = m // (HID // P), m % (HID // P)
                sp.dma_start(w2_s[:, m, (h % 2) * DO:(h % 2 + 1) * DO], W2[h, c * P:(c + 1) * P, :]).then_inc(s_weights, 16)
            for h in range(H):
                for u in range(2):
                    sp.dma_start(ad_s[(h % 2) * DO:(h % 2 + 1) * DO, h // 2, u, (h % 2) * AT:(h % 2 + 1) * AT],
                                 A1[h, u * DO:(u + 1) * DO, :]).then_inc(s_weights, 16)
            sp.dma_start(ab1_b, ab1.rearrange("(a h) n -> a (h n)", a=1).to_broadcast([P, ZW])).then_inc(s_weights, 16)
            sp.dma_start(a2_b[:, :], A2.rearrange("(a h) n b -> a (h n b)", a=1).to_broadcast([P, ZW])).then_inc(s_weights, 16)
            sp.dma_start(ab2_b[:, :], ab2.rearrange("(a h) n -> a (h n)", a=1).to_broadcast([P, H])).then_inc(s_weights, 16)
            sp.dma_start(a_row[0:1, :], A1[:, 2 * DO, :].rearrange("(a h) n -> a h n", a=1)).then_inc(s_weights, 16)
            sp.dma_start(b1_s, b1.rearrange("h (c p) -> p (h c)", p=P), allow_slow_non_contiguous=True).then_inc(s_weights, 16)
            for q in range(2):
                sp.dma_start(b2_s[:, q:q + 1], b2[2 * q:2 * q + 2, :].rearrange("r (d a) -> (r d) a", a=1),
                             allow_slow_non_contiguous=True).then_inc(s_weights, 16)
            sp.wait_ge(s_empty, 1)
            EW = SB * 4 * 16
            flat = records.rearrange("(p t) n -> p (t n)", p=P)
            for o in range(0, NT * 4, EW):
                n = min(EW, NT * 4 - o)
                sp.dma_start(flat[:, o:o + n], empty[:, 0:n]).then_inc(s_empty, 16)
            x_g = x.rearrange("(g w p) n -> g p w n", w=4, p=WN)
            p_g = p_table.rearrange("(g w p) n -> g w p n", w=4, p=WN)
            qf_g = qf_table.rearrange("(g w p) n -> g w p n", w=4, p=WN)

            def load_x(g):
                since(sp, s_xt_mm, g)
                sp.dma_start(x_rows[0:WN, :, :], x_g[group_at(g), :, :, :].rearrange("a p w n -> (a p) w n")).then_inc(s_x, 16)

            def store(g):
                for w in range(4):
                    sp.wait_ge(s_p_lo, g * 4 + w + 1)
                    sp.dma_start(p_g[group_at(g), w, :, :].rearrange("a p n -> (a p) n"), p_out[0:WN, w % 2, :]).then_inc(s_p_st[w % 2], 16)
                    sp.wait_ge(s_q_ev, g * 4 + w + 1)
                    sp.wait_ge(s_t_ev, g * 4 + w + 1)
                    sp.dma_start(qf_g[group_at(g), w, :, :].rearrange("a p n -> (a p) n"), qf_out[0:WN, w % 2, :]).then_inc(s_qf_st[w % 2], 16)

            def group(g):
                load_x(g + 1)
                store(g)

            load_x(0)
            loop(sp, GROUPS - 1, group)
            store(GROUPS - 1)
            for n in range(2):
                sp.wait_ge(s_p_st[n], 32 * GROUPS)
                sp.wait_ge(s_qf_st[n], 32 * GROUPS)
            sp.wait_ge(s_a_step, 5)
            for slot in range(2):
                for r in range(3):
                    sp.dma_start(p_win[WN + r:WN + r + 1, slot, :], a_parts[0:1, :]).then_inc(s_a_rows, 16)
            sp.wait_ge(s_a_rows, 16 * 6)
            sp.wait_ge(s_tab_step, N_TAB_STEPS)
            for n in range(SUBS):
                sp.wait_ge(s_scat[n], 16 * LOT * GROUPS)
            rec_d = records.rearrange("(p t) n -> p (t n)", p=P)
            sp.dma_start(rec_all[:, 0:RING * 4], rec_d[:, 0:RING * 4]).then_inc(s_rec_first, 16)
            sp.dma_start(rec_all[:, RING * 4:], rec_d[:, RING * 4:]).then_inc(s_rec_all, 16)
            sp.wait_ge(s_rec_first, 16)
            sp.sem_inc(s_start, 1)
            p_w = p_table.rearrange("(g v p) n -> g v p n", v=2, p=WN)
            with sp.Fori(0, W // 2) as g:
                for v in range(2):
                    done = sp.value_load(end_prev[0:1, bass.ds(g * 2 + v, 1)], min_val=1, max_val=NT + 1)
                    sp.wait_ge(s_z_mm, done)
                    sp.dma_start(p_win[0:WN, v, :], p_w[bass.ds(g, 1), v, :, :].rearrange("a p n -> (a p) n")).then_inc(s_win[v], 16)
                    sp.wait_ge(s_win[v], g * 16 + 16)
                    sp.sem_inc(s_win_ready, 1)
            x_c = x.rearrange("(g w p) n -> g p w n", w=CG, p=WN)
            sp.wait_ge(s_acc, NT)
            sp.wait_ge(s_shift_all, NSB)
            sp.dma_start(shift_rows.rearrange("(a s) h -> a (s h)", a=1), shift_flat[0:1, :]).then_inc(s_c_shifts, 16)
            sp.wait_ge(s_c_shifts, 16)
            sp.dma_start(c_shift[0:SC, :, :], shift_rows.rearrange("(k s) h -> s k h", s=SC),
                         allow_slow_non_contiguous=True).then_inc(s_c_shifts, 16)

            def load(i, k):
                if live_c(i, k, 0):
                    g = i * CR + k
                    since(sp, s_c_add, g - 1)
                    sp.dma_start(c_x[0:WN, k % 2, :, :], x_c[group_at(g), :, :, :].rearrange("a p w n -> (a p) w n")).then_inc(s_c_x[k % 2], 16)

            finish_pipeline(sp, load)
            for n in range(2):
                sp.wait_ge(s_c_out[n], 8 * CGROUPS)

        @block.gpsimd
        def _(pool):
            pool.memset(w2_s, 0.0).then_inc(s_const, 1)
            pool.memset(ad_s, 0.0).then_inc(s_const, 1)
            rec_w = empty.rearrange("p (t n) -> p t n", n=4)
            pool.memset(empty, 0.0).then_inc(s_const, 1)
            pool.wait_ge(s_const, 3)
            pool.memset(rec_w[:, :, 2:3].bitcast(BF16)[:, :, 1:2], LOW).then_inc(s_empty, 1)
            pool.memset(ones_f[:, :], 1.0).then_inc(s_const, 1)
            pool.memset(ones_b[:, :], 1.0).then_inc(s_const, 1)
            pool.memset(ident[:, :], 0.0).then_inc(s_const, 1)
            pool.memset(qf_out, 0.0).then_inc(s_const, 1)
            pool.memset(zeros_b, 0.0).then_inc(s_const, 1)
            pool.iota(iota_row[:, :], [[1, WN]], base=1, channel_multiplier=0, allow_small_or_imprecise_dtypes=True).then_inc(s_const, 1)
            pool.iota(iota_win[:, :, :], [[0, CH], [1, W]], base=0, channel_multiplier=0, allow_small_or_imprecise_dtypes=True).then_inc(s_const, 1)
            pool.iota(win_iota, [[P, NT]], base=0, channel_multiplier=0, allow_small_or_imprecise_dtypes=True).then_inc(s_const, 1)
            pool.wait_ge(s_const, 11)
            pool.affine_select(out=ident[:, :], in_=ident[:, :], pattern=[[-1, P]], compare_op=ALU.not_equal,
                               fill=1.0, base=0, channel_multiplier=1).then_inc(s_const, 1)
            pool.affine_select(out=before[:, :], in_=ones_b[:, :], pattern=[[1, P]], compare_op=ALU.is_ge,
                               fill=0.0, base=-1, channel_multiplier=-1).then_inc(s_const, 1)
            pool.memset(same_hi, 0.0).then_inc(s_masks, 1)
            pool.affine_select(out=same_col, in_=ones_f[:, 0:HCOL * LO].rearrange("p (c n) -> p c n", c=HCOL), pattern=[[-HI, HCOL], [0, LO]],
                               compare_op=ALU.is_ge, fill=0.0, base=0, channel_multiplier=1).then_inc(s_masks, 1)
            pool.wait_ge(s_masks, 2)
            pool.affine_select(out=same_col, in_=same_col, pattern=[[HI, HCOL], [0, LO]],
                               compare_op=ALU.is_ge, fill=0.0, base=HI - 1, channel_multiplier=-1).then_inc(s_masks, 1)
            for c in range(HCOL):
                pool.wait_ge(s_masks, 3 + c)
                pool.affine_select(out=same_hi, in_=same_hi, pattern=[[-1, HI], [0, LO]], compare_op=ALU.not_equal,
                                   fill=1.0, base=-HI * c, channel_multiplier=1).then_inc(s_masks, 1)
            pool.wait_ge(s_edges, 48)
            pool.wait_ge(s_edge_step, N_EDGE)
            R = rec_src[0:EP, :].rearrange("p (c n) -> p c n", n=4)
            RB = rec_src[0:EP, :].bitcast(BF16).rearrange("p (c n) -> p c n", n=8)
            ta, wt = tmp_a[0:EP, :], weight_f[0:EP, :]
            part_steps = [
                lambda: pool.tensor_copy(RB[:, :, 2], wt),
                lambda: pool.tensor_tensor(ta, wt, RB[:, :, 2], ALU.subtract),
                lambda: pool.tensor_copy(RB[:, :, 3], ta),
                lambda: pool.tensor_tensor(ta, ta, RB[:, :, 3], ALU.subtract),
                lambda: pool.tensor_copy(RB[:, :, 4], ta),
                lambda: pool.memset(RB[:, :, 5], 0.0),
                lambda: pool.tensor_copy(R[:, :, 3:4].bitcast(I32)[:, :, 0], dst_i[0:EP, :]),
            ]
            assert len(part_steps) == N_PARTS
            for n, op in enumerate(part_steps):
                if n:
                    pool.wait_ge(s_parts, n)
                op().then_inc(s_parts, 1)
            pool.wait_ge(s_empty, 1 + 16 * N_EMPTY)
            def scatter(g):
                for s in range(SUBS):
                    pool.wait_ge(s_at, g * 2 * SUBS + 2 * s + 2)
                    pool.sem_inc(s_passed, 1)
                    for c in range(LOT):
                        pool.indirect_dma_start(
                            out=records, out_offset=bass.IndirectOffsetOnAxis(ap=pos_at[0:EP, s, c:c + 1], axis=0),
                            in_=rec_out[0:EP, s, 4 * c:4 * c + 4], in_offset=None, compute_op=ALU.bypass).then_inc(s_scat[s], 16)
            loop(pool, GROUPS, scatter)
            pool.wait_ge(s_start, 1)

            rec_b = rec[:, :, :].bitcast(BF16)

            def step(i, k):
                def tile(off, j):
                    return i * RING + (k + off) * SB + j

                def take_records():
                    o = (k + 2) % SPB * SB
                    if isinstance(i, int) and (i, k) == (0, 2):
                        pool.wait_ge(s_rec_all, 16)
                    if live(i, k, -2):
                        pool.wait_ge(s_tmax, i * SPB + k - 1)
                    pool.tensor_copy(rec[:, o:o + SB, :], rec_words[:, bass.ds(tile(2, 0), SB), :]).then_inc(s_rec, 1)
                    pool.wait_ge(s_rec, i * SPB + k + 3)
                    pool.tensor_tensor(bias_mask[:, o:o + SB, :], ab2_b[:, :].unsqueeze(1).to_broadcast([P, SB, H]),
                                       rec_b[:, o:o + SB, 5:6].to_broadcast([P, SB, H]), ALU.add).then_inc(s_bias_mask, 1)

                def keep_shift():
                    pool.wait_ge(s_shift, i * SPB + (k - 1))
                    pool.sem_inc(s_passed, 1)
                    pool.tensor_copy(shift_all[:, bass.ds(i * SPB + (k - 2), 1), :].rearrange("p a h -> p (a h)"),
                                     shift[:, (k - 2) % SPB, :]).then_inc(s_shift_all, 1)

                def gather(j):
                    slot = ((k + 1) * SB + j) % RING
                    if j == 0:
                        pool.wait_ge(s_rec, i * SPB + k + 2)
                    if live(i, k, -3):
                        pool.wait_ge(s_agg, tile(-3, j) + 1)
                    pool.sem_inc(s_passed, 1)
                    pool.memset(z_t[:, slot, ZW:QW], 0.0).then_inc(s_z_zero, 1)
                    pool.wait_ge(s_z_zero, tile(1, j) + 1)
                    pool.wait_ge(s_z_ev, tile(1, j) + 1)
                    pool.sem_inc(s_passed, 1)
                    pool.indirect_dma_start(
                        out=z_t[:, slot, :], out_offset=None, in_=qf_table,
                        in_offset=bass.IndirectOffsetOnAxis(ap=rec[:, slot, 3:4].bitcast(I32), axis=0),
                        compute_op=ALU.add).then_inc(s_gather[slot], 16)

                def weight_last():
                    zf = z_t[:, ((k - 1) * SB + SB - 1) % RING, ZW:QW].rearrange("p (h f) -> p h f", f=HF)
                    pool.wait_ge(s_w, i * SPB + k)
                    pool.sem_inc(s_passed, 1)
                    pool.tensor_tensor(zf[:, :, 0:DO], zf[:, :, 0:DO], zf[:, :, DO:HF].to_broadcast([P, H, DO]), ALU.mult)\
                        .then_inc(s_wf_last, 1)

                if live(i, k, 2):
                    take_records()
                if live(i, k, 1):
                    gather(0)
                if live(i, k, -2):
                    keep_shift()
                if live(i, k, 1):
                    gather(1)
                if live(i, k, -1):
                    weight_last()
                if live(i, k, 1):
                    gather(2)
                if live(i, k, 1):
                    gather(3)

            pipeline(pool, step)

            pool.wait_ge(s_acc, NT)
            pool.wait_ge(s_shift_all, NSB)
            pool.memset(c_eps, EPS).then_inc(s_c_const, 1)
            pool.iota(c_id, [[SC, KS]], base=0, channel_multiplier=1, allow_small_or_imprecise_dtypes=True).then_inc(s_c_const, 1)

            def add_x(i, k):
                if live_c(i, k, 0):
                    g = i * CR + k
                    pool.wait_ge(s_c_y, g + 1)
                    pool.wait_ge(s_c_x[k % 2], i * (8 * CR) + (k // 2 + 1) * 16)
                    pool.sem_inc(s_passed, 1)
                    pool.tensor_tensor(c_y[0:WN, k, :, :], c_y[0:WN, k, :, :], c_x[0:WN, k % 2, :, :], ALU.add).then_inc(s_c_add, 1)

            finish_pipeline(pool, add_x)

        @block.tensor
        def _(pe):
            pe.wait_ge(s_const, 13)
            pe.matmul(psum[:, 0, 0:HCOL * LO], zeros_b, ones_b[:, 0:HCOL * LO], start=True, stop=False,
                      skip_group_check=True).then_inc(s_hist, 1)

            def count_windows(g):
                for b in range(2):
                    pe.wait_ge(s_hist_oh, g * 2 + b + 1)
                    for c in range(0, HB, HCOL):
                        mm = pe.matmul(psum[:, 0, 0:HCOL * LO], hi_oh[0:EP, b, c:c + HCOL, :].rearrange("p c n -> p (c n)"),
                                       lo_oh[0:EP, b, c:c + HCOL, :].rearrange("p c n -> p (c n)"),
                                       start=False, stop=False, skip_group_check=True)
                    mm.then_inc(s_hist, 1)

            loop(pe, EC // (2 * HB), count_windows)
            pe.wait_ge(s_fold, 3)
            pe.matmul(psum[:, 1, 0:HI * LO], ones_f[:, :], by_hi.rearrange("p h n -> p (h n)"), start=True, stop=True).then_inc(s_fold_mm, 1)
            pe.wait_ge(s_weights, N_W)
            pe.wait_ge(s_base, 1)
            pe.sem_inc(s_count, 1)

            def prefix(g, q):
                n = g * (CPI // CH) + q
                pe.wait_ge(s_oh, n + 1)
                since(pe, s_carry, n)
                o = psum[:, q % 2, :]
                for c in range(CH):
                    oh = win_oh[0:EP, q % 2, c, :]
                    pe.matmul(o[:, (c + 1) * W:(CH + 1) * W].rearrange("p (c w) -> p c w", w=W), ones_b[0:EP, :],
                              oh.unsqueeze(1).to_broadcast([EP, CH - c, W]), start=(c == 0), stop=False, skip_group_check=True)
                    mm = pe.matmul(o[:, c * W:(c + 1) * W], before[0:EP, :], oh, start=False, stop=(c == CH - 1),
                                   skip_group_check=True)
                mm.then_inc(s_count, 1)

            def hidden(g, m):
                since(pe, s_h_ev, g * MC + max(m - 1, 0))
                if m == 0:
                    pe.wait_ge(s_xt, g * KC + KC)
                    since(pe, s_q_ev, g * 4)
                h, c = m // (HID // P), m % (HID // P)
                for k in range(KC):
                    mm = pe.matmul(psum[:, 2 + m % 2, 0:NG], w1_s[:, k, h, c * P:(c + 1) * P], x_t[:, k, :],
                                   start=(k == 0), stop=(k == KC - 1))
                mm.then_inc(s_h_mm, 1)

            def feats(g, q):
                if q:
                    pe.wait_ge(s_f_ev, g * 2 + 1)
                for m in range(MC // 2 * q, MC // 2 * (q + 1)):
                    pe.wait_ge(s_h_ev, g * MC + m + 1)
                    mm = pe.matmul(psum[:, 4, 0:NG], w2_s[:, m, :], h_t[:, m, :], start=(m == MC // 2 * q),
                                   stop=(m == MC // 2 * (q + 1) - 1))
                mm.then_inc(s_f_mm, 1)

            def window(g, w):
                n = g * 4 + w
                at = slice(w * WN, (w + 1) * WN)
                if w == 0:
                    pe.wait_ge(s_f_ev, g * 2 + 2)
                    pe.wait_ge(s_h_ev, g * MC + MC)
                since(pe, s_p_ev, n)
                for q in range(2):
                    mm = pe.matmul(psum[0:WN, 5 + q, 0:HALF], f_t[:, q, at], ad_s[:, q, 0, :], start=True, stop=True)
                mm.then_inc(s_p_mm, 1)
                since(pe, s_t_ev, n)
                for q in range(2):
                    mm = pe.transpose(psum[0:WN, 7, q * P:(q + 1) * P], f_t[:, q, at], ident[:, :])
                mm.then_inc(s_t_mm, 1)
                since(pe, s_q_ev, n)
                for q in range(2):
                    mm = pe.matmul(psum[0:WN, 2 + q, 0:HALF], f_t[:, q, at], ad_s[:, q, 1, :], start=True, stop=True)
                mm.then_inc(s_q_mm, 1)

            beside = {0: [], 1: [(hidden, 0)], 2: [(hidden, 1), (hidden, 2)], 3: [(hidden, 3)], 4: [(hidden, 4), (hidden, 5)],
                      5: [(hidden, 6)], 6: [(hidden, 7)], 7: [(feats, 0)], 8: [(feats, 1)],
                      9: [(window, 0)], 11: [(window, 1)], 13: [(window, 2)], 15: [(window, 3)]}
            assert MC == 8 and CPI // CH == 16

            def group(g):
                pe.wait_ge(s_x, g * 16 + 16)
                since(pe, s_t_ev, g * 4)
                since(pe, s_f_ev, g * 2)
                for c in range(KC):
                    for w in range(4):
                        mm = pe.transpose(psum[:, [7, 4][c], w * WN:(w + 1) * WN], x_rows[0:WN, w, c * P:(c + 1) * P],
                                          ident[0:WN, 0:WN])
                mm.then_inc(s_xt_mm, 1)
                for q in range(CPI // CH):
                    prefix(g, q)
                    for product, n in beside.get(q, []):
                        product(g, n)
            loop(pe, GROUPS, group)
            pe.wait_ge(s_carry, EC // CH + 1)
            pe.wait_ge(s_q_ev, GROUPS * 4)
            pe.wait_ge(s_p_ev, GROUPS * 4)
            pe.wait_ge(s_base, 4)
            pe.matmul(psum[0:W, 1, 0:1], ends[0:1, :], ones_f[0:1, 0:1], start=True, stop=True).then_inc(s_tab_mm, 1)
            pe.wait_ge(s_base, 6)
            for n, o in enumerate(range(0, NT, 512)):
                m = min(512, NT - o)
                pe.matmul(psum[0:1, 2 + n, 0:m], ones_b[0:W, 0:1], win_done[0:W, o:o + m], start=True, stop=True).then_inc(s_tab_mm, 1)
            pe.wait_ge(s_start, 1)
            pe.sem_inc(s_z_mm, 1)

            def z_parts(t, slot, w):
                pe.wait_ge(s_win_ready, w + 1)
                for half in range(2):
                    for part in range(3):
                        mm = pe.matmul(psum[:, slot % 2 * 2 + half, 0:HALF], onehot_t[:, slot % (RING // 2), :],
                                       p_flat[:, bass.ds((w % 2) * (3 * ZW) + (part * ZW + half * HALF), HALF)],
                                       start=(part == 0), stop=(part == 2))
                mm.then_inc(s_z_mm, 1)

            def step(i, k):
                def tile(off, j):
                    return i * RING + (k + off) * SB + j

                def sum_up(off, j):
                    t, slot = tile(off, j), ((k + off) * SB + j) % RING
                    if j == SB - 1:
                        pe.wait_ge(s_wf_last, i * SPB + (k + off) + 1)
                    else:
                        pe.wait_ge(s_wf, (i * SPB + (k + off)) * (SB - 1) + (j + 1))
                    since(pe, s_acc, t - 1)
                    pe.matmul(psum[:, 4 + slot % 2, 0:H * HF], onehot[:, slot, :], z_t[:, slot, ZW:QW], start=True, stop=True)\
                      .then_inc(s_agg, 1)

                def hidden_src(j):
                    slot = ((k + 1) * SB + j) % RING
                    w = win_at(pack, j)
                    if j == 0:
                        pe.wait_ge(s_oht, i * SPB + k + 2)
                    since(pe, s_z_ev, tile(1, j) - 1)
                    z_parts(tile(1, j), slot, w)

                def turn():
                    pe.wait_ge(s_onehot, i * SPB + k + 3)
                    if live(i, k, 1):
                        pe.wait_ge(s_oht, i * SPB + k + 2)
                    for j in range(SB):
                        mm = pe.transpose(psum[:, 6, j * P:(j + 1) * P], onehot[:, ((k + 2) * SB + j) % RING, :], ident[:, :])
                    mm.then_inc(s_oht_mm, 1)

                def max_t():
                    pe.wait_ge(s_tmax, i * SPB + k)
                    pe.transpose(psum[0:H, 7, 0:P], tile_max[:, (k - 1) % SPB, :], ident[:, :]).then_inc(s_tmax_t, 1)

                def max_to_all():
                    pe.wait_ge(s_diag, i * SPB + k)
                    pe.matmul(psum[:, 7, P:P + H], ones_f[0:H, :], max_diag[:, (k - 1) % SPB, :], start=True, stop=True)\
                      .then_inc(s_max_b, 1)

                if live(i, k, 1):
                    pack = pe.value_load(win_pack[0:1, bass.ds(i * SPB + (k + 1), 1)], min_val=0, max_val=(1 << 28) - 1)
                if live(i, k, -2):
                    sum_up(-2, 1)
                if live(i, k, 1):
                    hidden_src(0)
                if live(i, k, -1):
                    max_t()
                if live(i, k, -2):
                    sum_up(-2, 2)
                if live(i, k, 1):
                    hidden_src(1)
                if live(i, k, -1):
                    max_to_all()
                if live(i, k, -2):
                    sum_up(-2, 3)
                if live(i, k, 1):
                    hidden_src(2)
                if live(i, k, -1):
                    sum_up(-1, 0)
                if live(i, k, 2):
                    turn()
                if live(i, k, 1):
                    hidden_src(3)

            pipeline(pe, step)

            pe.wait_ge(s_c_pick, KS)
            for k in range(KS):
                mm = pe.matmul(psum[:, 0, 0:W * H], ones_f[0:SC, :], c_pick[0:SC, k, :, :].rearrange("p w h -> p (w h)"),
                               start=(k == 0), stop=(k == KS - 1))
            mm.then_inc(s_c_factor, 1)

        @block.scalar
        def _(act):
            act.wait_ge(s_weights, N_W)
            def group(g):
                act.wait_ge(s_xt_mm, g + 1)
                since(act, s_h_mm, g * MC)
                for c in range(KC):
                    act.activation(x_t[:, c, :], psum[:, [7, 4][c], 0:NG], ACT.Copy).then_inc(s_xt, 1)
                since(act, s_f_mm, g * 2)
                for m in range(MC):
                    act.wait_ge(s_h_mm, g * MC + m + 1)
                    act.activation(h_t[:, m, :], psum[:, 2 + m % 2, 0:NG], ACT.Relu, bias=b1_s[:, m:m + 1]).then_inc(s_h_ev, 1)
                since(act, s_q_mm, g * 4)
                for q in range(2):
                    act.wait_ge(s_f_mm, g * 2 + q + 1)
                    act.activation(f_t[:, q, :], psum[:, 4, 0:NG], ACT.Identity, bias=b2_s[:, q:q + 1]).then_inc(s_f_ev, 1)
                for w in range(4):
                    n = g * 4 + w
                    act.wait_ge(s_p_ev, n + 1)
                    since(act, s_p_st[w % 2], g * 32 + w // 2 * 16)
                    act.activation(p_out[0:WN, w % 2, 0:ZW], p_f[0:WN, :], ACT.Copy).then_inc(s_p_hi, 1)
                    act.wait_ge(s_q_mm, n + 1)
                    since(act, s_qf_st[w % 2], g * 32 + w // 2 * 16)
                    act.activation(qf_out[0:WN, w % 2, 0:ZW].rearrange("p (q n) -> p q n", q=2), psum[0:WN, 2:4, 0:HALF],
                                   ACT.Copy).then_inc(s_q_ev, 1)
                    act.wait_ge(s_p_rest, n + 1)
                    act.activation(p_out[0:WN, w % 2, ZW:2 * ZW], p_f[0:WN, :], ACT.Copy).then_inc(s_p_mid, 1)
            loop(act, GROUPS, group)
            act.wait_ge(s_start, 1)

            def step(i, k):
                def tile(off, j):
                    return i * RING + (k + off) * SB + j

                def weight(off, j):
                    slot = ((k + off) * SB + j) % RING
                    act.wait_ge(s_w, i * SPB + (k + off) + 1)
                    for h in range(H):
                        o = ZW + h * HF
                        op = act.activation(z_t[:, slot, o:o + DO], z_t[:, slot, o:o + DO], ACT.Copy, scale=z_t[:, slot, o + DO:o + HF])
                    op.then_inc(s_wf, 1)

                def take_hidden(j):
                    slot = ((k + 1) * SB + j) % RING
                    act.wait_ge(s_z_mm, tile(1, j) + 2)
                    if live(i, k, -3):
                        act.wait_ge(s_agg, tile(-3, j) + 1)
                    act.activation(z_t[:, slot, 0:ZW].rearrange("p (q n) -> p q n", q=2),
                                   psum[:, slot % 2 * 2:slot % 2 * 2 + 2, 0:HALF], ACT.Copy).then_inc(s_z_ev, 1)

                def exps():
                    o, kk = (k - 1) % SPB * SB, (k - 1) % SPB
                    act.wait_ge(s_esh, i * SPB + k)
                    act.activation(z_t[:, o:o + SB, ZW:QW].rearrange("p t (h f) -> p t h f", f=HF)[:, :, :, DO],
                                   e_sh[:, o:o + SB, :], ACT.Exp).then_inc(s_w, 1)
                    act.wait_ge(s_drop, i * SPB + k)
                    act.activation(decay[:, kk, :], drop[:, kk, :], ACT.Exp).then_inc(s_decay, 1)

                def take_turned():
                    o = k % 2 * SB
                    act.wait_ge(s_oht_mm, i * SPB + k + 3)
                    if live(i, k, 0):
                        act.wait_ge(s_z_mm, tile(0, SB - 1) + 2)
                    act.activation(onehot_t[:, o:o + SB, :].rearrange("p t n -> p (t n)"), psum[:, 6, :], ACT.Copy).then_inc(s_oht, 1)

                if live(i, k, -2):
                    weight(-2, 2)
                if live(i, k, 1):
                    take_hidden(0)
                if live(i, k, 1):
                    take_hidden(1)
                if live(i, k, -1):
                    exps()
                if live(i, k, -1):
                    weight(-1, 0)
                if live(i, k, 1):
                    take_hidden(2)
                if live(i, k, -1):
                    weight(-1, 1)
                if live(i, k, 2):
                    take_turned()
                if live(i, k, 1):
                    take_hidden(3)

            pipeline(act, step)
            act.wait_ge(s_c_diff, 1)
            act.activation(c_exp[0:SC], c_shift[0:SC], ACT.Exp).then_inc(s_c_exp, 1)
            act.wait_ge(s_c_const, 2)
            o_c = out.rearrange("(g w p) n -> g p w n", w=CG, p=WN)

            def scale(i, k):
                g = i * CR + k
                if live_c(i, k, -1):
                    b = (k - 1) % CR
                    act.wait_ge(s_c_var, g)
                    act.activation(c_sd[0:WN, b, :], c_mv[0:WN, b, :, 1], ACT.Sqrt, bias=c_eps[0:WN, :]).then_inc(s_c_std, 1)
                if live_c(i, k, -2):
                    b = (k - 2) % CR
                    act.wait_ge(s_c_bias, g - 1)
                    since(act, s_c_out[k % 2], i * (8 * CR) + (k - 2) // 2 * 16)
                    for v in range(CG):
                        op = act.activation(c_o[0:WN, k % 2, v, :], c_y[0:WN, b, v, :], ACT.Identity,
                                            scale=c_is[0:WN, b, v:v + 1], bias=c_nb[0:WN, b, v:v + 1])
                    op.then_inc(s_c_ready, 1)
                    act.wait_ge(s_c_ready, g - 1)
                    act.dma_start(o_c[group_at(g - 2), :, :, :].rearrange("a p w n -> (a p) w n"), c_o[0:WN, k % 2, :, :]).then_inc(s_c_out[k % 2], 16)

            finish_pipeline(act, scale)

        @block.vector
        def _(dve):
            R = rec_src[0:EP, :].rearrange("p (c n) -> p c n", n=4)
            R0, R1, R2 = (R[:, :, n] for n in range(3))
            R1I, R2I = (R[:, :, n:n + 1].bitcast(I32)[:, :, 0] for n in (1, 2))
            ta = tmp_a[0:EP, :]
            dve.wait_ge(s_edges, 48)
            edge_steps = [
                lambda: dve.tensor_copy(ta, src_i[0:EP, :]),
                lambda: dve.tensor_scalar(R1I, ta, 1.0 / WN, None, ALU.mult),
                lambda: dve.tensor_copy(R2, R1I),
                lambda: dve.scalar_tensor_tensor(out=R0, in0=R2, scalar=-float(WN), in1=ta, op0=ALU.mult, op1=ALU.add),
                lambda: dve.tensor_scalar(R1, R0, 0.0, None, ALU.is_lt),
                lambda: dve.tensor_tensor(edge_win[0:EP, :], R2, R1, ALU.subtract),
                lambda: dve.scalar_tensor_tensor(out=R0, in0=R1, scalar=float(WN), in1=R0, op0=ALU.mult, op1=ALU.add),
                lambda: dve.tensor_scalar(R0, R0, 1.0, None, ALU.add),
                lambda: dve.tensor_copy(R1I, edge_win[0:EP, :]),
                lambda: dve.tensor_scalar(R2I, R1I, LO.bit_length() - 1, None, ALU.logical_shift_right),
                lambda: dve.tensor_copy(edge_hi[0:EP, :], R2I),
                lambda: dve.tensor_scalar(R2I, R1I, LO - 1, None, ALU.bitwise_and),
                lambda: dve.tensor_copy(edge_lo[0:EP, :], R2I),
            ]
            for n, op in enumerate(edge_steps):
                if n:
                    dve.wait_ge(s_edge_step, n)
                op().then_inc(s_edge_step, 1)
            dve.wait_ge(s_const, 13)
            assert len(edge_steps) == N_EDGE
            dve.wait_ge(s_edge_step, N_EDGE)

            def edge_onehot(g, c, b):
                return dve.tensor_tensor(win_oh[0:EP, b, :, :],
                                         edge_win[0:EP, bass.ds(g * CPI + c, CH)].unsqueeze(2).to_broadcast([EP, CH, W]),
                                         iota_win[0:EP, :, :], ALU.is_equal)

            def count_windows(g):
                for b in range(2):
                    since(dve, s_hist, g * 2 + b)
                    for oh, digit, n in ((hi_oh, edge_hi, HI), (lo_oh, edge_lo, LO)):
                        op = dve.tensor_tensor(oh[0:EP, b, :, :],
                                               digit[0:EP, bass.ds((g * 2 + b) * HB, HB)].unsqueeze(2).to_broadcast([EP, HB, n]),
                                               iota_win[0:EP, 0:1, 0:n].to_broadcast([EP, HB, n]), ALU.is_equal)
                    op.then_inc(s_hist_oh, 1)

            loop(dve, EC // (2 * HB), count_windows)
            dve.wait_ge(s_hist, EC // HB + 1)
            dve.wait_ge(s_masks, 3 + HCOL)
            dve.tensor_tensor(by_col, psum[:, 0, 0:HCOL * LO].rearrange("p (c n) -> p c n", c=HCOL), same_col, ALU.mult).then_inc(s_fold, 1)
            dve.wait_ge(s_fold, 1)
            dve.tensor_reduce(by_lo, by_col.rearrange("p c n -> p n c"), AX_X, ALU.add).then_inc(s_fold, 1)
            dve.wait_ge(s_fold, 2)
            dve.tensor_tensor(by_hi, same_hi, by_lo.unsqueeze(1).to_broadcast([P, HI, LO]), ALU.mult).then_inc(s_fold, 1)
            dve.wait_ge(s_fold_mm, 1)
            dve.tensor_copy(counts[:, :], psum[:, 1, 0:W]).then_inc(s_base, 1)
            dve.wait_ge(s_base, 1)
            dve.tensor_scalar(sizes_i[:, :], counts[:, :], float(P - 1), None, ALU.add).then_inc(s_base, 1)
            dve.wait_ge(s_base, 2)
            dve.tensor_scalar(sizes_i[:, :], sizes_i[:, :], -P, None, ALU.bitwise_and).then_inc(s_base, 1)
            dve.wait_ge(s_base, 3)
            dve.tensor_copy(sizes[:, :], sizes_i[:, :]).then_inc(s_tab_step, 1)
            dve.wait_ge(s_tab_step, 1)
            dve.tensor_tensor_scan(ends[:, :], ones_f[:, 0:W], sizes[:, :], 0.0, ALU.mult, ALU.add).then_inc(s_base, 1)
            dve.wait_ge(s_base, 4)
            dve.tensor_tensor(count_t[:, 1, CH * W:(CH + 1) * W], ends[:, :], sizes[:, :], ALU.subtract).then_inc(s_tab_step, 1)
            dve.wait_ge(s_parts, N_PARTS)
            dve.wait_ge(s_tab_step, 2)
            dve.sem_inc(s_carry, 1)

            def picked(g, s, q):
                n = s * CHUNKS + q
                return g * (SUBS * (CHUNKS + 3)) + (n + 1 + n // CHUNKS * 3)

            def sort_onehot(g, s, q):
                n = g * (CPI // CH) + s * CHUNKS + q
                since(dve, s_count, n)
                since(dve, s_pos, picked(g, s, q - 2))
                edge_onehot(g, s * LOT + q * CH, q % 2).then_inc(s_oh, 1)

            def sort_pick(g, s, q):
                n = g * (CPI // CH) + s * CHUNKS + q
                dve.wait_ge(s_count, n + 2)
                dve.wait_ge(s_carry, n + 1)
                since(dve, s_pos, picked(g, s, q - 2))
                dve.tensor_tensor(count_t[:, q % 2, :].rearrange("p (c w) -> p c w", w=W),
                                  psum[:, q % 2, 0:(CH + 1) * W].rearrange("p (c w) -> p c w", w=W),
                                  count_t[:, (q + 1) % 2, CH * W:].unsqueeze(1).to_broadcast([P, CH + 1, W]), ALU.add).then_inc(s_carry, 1)
                dve.wait_ge(s_carry, n + 2)
                for c in range(CH):
                    own = count_t[0:EP, q % 2, c * W:(c + 1) * W]
                    op = dve.scalar_tensor_tensor(out=own, in0=own, scalar=1.0,
                                                  in1=win_oh[0:EP, q % 2, c, :], op0=ALU.mult, op1=ALU.mult,
                                                  accum_out=pos_f[0:EP, s, q * CH + c:q * CH + c + 1])
                op.then_inc(s_pos, 1)

            def sort_places(g, s):
                n = picked(g, s, CHUNKS - 1)
                dve.wait_ge(s_pos, n)
                since(dve, s_at, (g * SUBS + s) * 2)
                dve.tensor_copy(pos_i[0:EP, s, :], pos_f[0:EP, s, :]).then_inc(s_pos, 1)
                dve.wait_ge(s_pos, n + 1)
                dve.tensor_scalar(pos_p[0:EP, :], pos_i[0:EP, s, :], P - 1, None, ALU.bitwise_and).then_inc(s_pos, 1)
                dve.tensor_scalar(pos_t[0:EP, :], pos_i[0:EP, s, :], 7, None, ALU.logical_shift_right).then_inc(s_pos, 1)
                dve.wait_ge(s_pos, n + 3)
                since(dve, s_scat[s], g * (16 * LOT))
                dve.scalar_tensor_tensor(out=pos_at[0:EP, s, :], in0=pos_p[0:EP, :], scalar=float(NT), in1=pos_t[0:EP, :],
                                         op0=ALU.mult, op1=ALU.add).then_inc(s_at, 1)
                dve.tensor_copy(rec_out[0:EP, s, :].bitcast(I32),
                                rec_src[0:EP, bass.ds((g * CPI + s * LOT) * 4, LOT * 4)].bitcast(I32)).then_inc(s_at, 1)

            pf = p_f[0:WN, :]

            def p_sum(g, w):
                n, b = g * 4 + w, w % 2
                dve.wait_ge(s_p_mm, n + 1)
                since(dve, s_p_lo, n)
                dve.tensor_tensor(pf.rearrange("p (q n) -> p q n", q=2), psum[0:WN, 5:7, 0:HALF],
                                  ab1_b[0:WN, :].rearrange("p (q n) -> p q n", q=2), ALU.add).then_inc(s_p_ev, 1)
                dve.wait_ge(s_t_mm, n + 1)
                since(dve, s_qf_st[b], g * 32 + w // 2 * 16)
                dve.tensor_copy(qf_out[0:WN, b, ZW:QW].rearrange("p (h f) -> p h f", f=HF)[:, :, 0:DO],
                                psum[0:WN, 7, 0:H * DO].rearrange("p (h f) -> p h f", h=H)).then_inc(s_t_ev, 1)

            def p_rest(g, w):
                n, b = g * 4 + w, w % 2
                dve.wait_ge(s_p_hi, n + 1)
                dve.tensor_tensor(pf, pf, p_out[0:WN, b, 0:ZW], ALU.subtract).then_inc(s_p_rest, 1)

            def p_last(g, w):
                n, b = g * 4 + w, w % 2
                dve.wait_ge(s_p_mid, n + 1)
                dve.wait_ge(s_p_rest, n + 1)
                dve.tensor_tensor(p_out[0:WN, b, 2 * ZW:3 * ZW], pf, p_out[0:WN, b, ZW:2 * ZW], ALU.subtract).then_inc(s_p_lo, 1)

            beside = {10: [(p_sum, 0)], 11: [(p_rest, 0)], 12: [(p_last, 0), (p_sum, 1)], 13: [(p_rest, 1)],
                      14: [(p_last, 1), (p_sum, 2)], 15: [(p_rest, 2), (p_last, 2), (p_sum, 3), (p_rest, 3), (p_last, 3)]}

            def group(g):
                for n in range(SUBS * CHUNKS + 1):
                    if n < SUBS * CHUNKS:
                        sort_onehot(g, n // CHUNKS, n % CHUNKS)
                    if n:
                        sort_pick(g, (n - 1) // CHUNKS, (n - 1) % CHUNKS)
                        if n % CHUNKS == 0:
                            sort_places(g, (n - 1) // CHUNKS)
                        for work, w in beside.get(n - 1, []):
                            work(g, w)
            loop(dve, GROUPS, group)
            dve.wait_ge(s_tab_mm, 1)
            dve.tensor_copy(end_col[0:W, :], psum[0:W, 1, 0:1]).then_inc(s_base, 1)
            dve.wait_ge(s_base, 5)
            dve.tensor_scalar(win_done[0:W, :], win_iota[0:W, :], end_col[0:W, :], None, ALU.is_ge).then_inc(s_base, 1)
            for n, o in enumerate(range(0, NT, 512)):
                m = min(512, NT - o)
                dve.wait_ge(s_tab_mm, n + 2)
                dve.tensor_scalar(win_of[:, o:o + m], psum[0:1, 2 + n, 0:m], float(W - 1), None, ALU.min).then_inc(s_base, 1)
            dve.wait_ge(s_base, 6 + N_TAB)
            quarter = win_of[:, :].rearrange("p (s j) -> p j s", j=SB)
            table_steps = [
                lambda: dve.tensor_copy(win_pack[:, :], quarter[:, 0, :]),
                lambda: dve.tensor_scalar(row_tmp[:, 0:NSB], quarter[:, 1, :], 7, None, ALU.logical_shift_left),
                lambda: dve.tensor_tensor(win_pack[:, :], win_pack[:, :], row_tmp[:, 0:NSB], ALU.bitwise_or),
                lambda: dve.tensor_scalar(row_tmp[:, 0:NSB], quarter[:, 2, :], 14, None, ALU.logical_shift_left),
                lambda: dve.tensor_tensor(win_pack[:, :], win_pack[:, :], row_tmp[:, 0:NSB], ALU.bitwise_or),
                lambda: dve.tensor_scalar(row_tmp[:, 0:NSB], quarter[:, 3, :], 21, None, ALU.logical_shift_left),
                lambda: dve.tensor_tensor(win_pack[:, :], win_pack[:, :], row_tmp[:, 0:NSB], ALU.bitwise_or),
                lambda: dve.memset(end_prev[:, :], 1),
                lambda: dve.tensor_scalar(end_prev[:, 2:W], ends[0:1, 0:W - 2], 1.0 / P, 1.0, ALU.mult, ALU.add),
                lambda: dve.tensor_scalar(sizes[:, :], ends[:, :], 1.0 / P, -1.0, ALU.mult, ALU.add),
                lambda: dve.tensor_scalar(last_sb[:, :], sizes[:, :], 0.0, None, ALU.max),
                lambda: dve.tensor_scalar(last_sb[:, :], last_sb[:, :], 2, None, ALU.logical_shift_right),
                lambda: dve.memset(last_sb[:, W - 1:W], NSB - 1),
            ]
            for n, op in enumerate(table_steps):
                dve.wait_ge(s_tab_step, n + 2)
                op().then_inc(s_tab_step, 1)
            assert len(table_steps) + 2 == N_TAB_STEPS
            dve.wait_ge(s_weights, N_W)
            ar, rest, ap3 = a_row[0:1, :], a_rest[0:1, :], a_parts[0:1, :].rearrange("p (u n) -> p u n", u=3)
            dve.tensor_copy(ap3[:, 0, :], ar).then_inc(s_a_step, 1)
            dve.wait_ge(s_a_step, 1)
            dve.tensor_tensor(rest, ar, ap3[:, 0, :], ALU.subtract).then_inc(s_a_step, 1)
            dve.wait_ge(s_a_step, 2)
            dve.tensor_copy(ap3[:, 1, :], rest).then_inc(s_a_step, 1)
            dve.wait_ge(s_a_step, 3)
            dve.tensor_tensor(rest, rest, ap3[:, 1, :], ALU.subtract).then_inc(s_a_step, 1)
            dve.wait_ge(s_a_step, 4)
            dve.tensor_copy(ap3[:, 2, :], rest).then_inc(s_a_step, 1)

            dve.wait_ge(s_q_ev, 4 * GROUPS)
            for n in range(2):
                dve.wait_ge(s_p_st[n], 32 * GROUPS)
                dve.wait_ge(s_qf_st[n], 32 * GROUPS)
            dve.wait_ge(s_a_rows, 16 * 6)
            dve.memset(acc[:, :], 0.0).then_inc(s_acc_zero, 1)
            dve.memset(shift[:, SPB - 1, :], LOW).then_inc(s_acc_zero, 1)
            dve.wait_ge(s_acc_zero, 2)
            dve.wait_ge(s_start, 1)
            rec_b = rec[:, :, :].bitcast(BF16)

            def step(i, k):
                def tile(off, j):
                    return i * RING + (k + off) * SB + j

                def sbn(off):
                    return i * SPB + (k + off)

                if live(i, k, -2):
                    pack = dve.value_load(win_pack[0:1, bass.ds(sbn(-2), 1)], min_val=0, max_val=(1 << 28) - 1)
                kk, kp, o = (k - 1) % SPB, (k - 2) % SPB, (k - 1) % SPB * SB
                ev, er = e_val[:, o:o + SB, :], e_raw[:, o:o + SB, :]

                def bias():
                    dve.wait_ge(s_dot, tile(-1, SB - 1) + 1)
                    dve.wait_ge(s_bias_mask, sbn(0))
                    dve.tensor_tensor(ev, er, bias_mask[:, o:o + SB, :], ALU.add).then_inc(s_e_bias, 1)

                def leaky():
                    dve.wait_ge(s_e_bias, sbn(0))
                    dve.scalar_tensor_tensor(out=ev, in0=ev, scalar=0.2, in1=ev, op0=ALU.mult, op1=ALU.max).then_inc(s_e_leaky, 1)

                def tiles_max():
                    dve.wait_ge(s_e_leaky, sbn(0))
                    dve.tensor_reduce(tile_max[:, kk, :], ev.rearrange("p t h -> p h t"), AX_X, ALU.max).then_inc(s_tmax, 1)

                def heads_max():
                    dve.wait_ge(s_tmax_t, sbn(0))
                    dve.tensor_reduce(head_max[:, kk:kk + 1], psum[0:H, 7, 0:P], AX_X, ALU.max).then_inc(s_head_max, 1)

                def diagonal():
                    dve.wait_ge(s_head_max, sbn(0))
                    dve.tensor_scalar(max_diag[:, kk, :], ident[0:H, 0:H], head_max[:, kk:kk + 1], None, ALU.mult).then_inc(s_diag, 1)

                def new_shift():
                    dve.wait_ge(s_max_b, sbn(0))
                    since(dve, s_shift, sbn(-1))
                    dve.tensor_tensor(shift[:, kk, :], psum[:, 7, P:P + H], shift[:, kp, :], ALU.max).then_inc(s_shift, 1)

                def shifted():
                    dve.wait_ge(s_shift, sbn(0))
                    dve.tensor_tensor(e_sh[:, o:o + SB, :], ev,
                                      shift[:, kk, :].unsqueeze(1).to_broadcast([P, SB, H]), ALU.subtract).then_inc(s_esh, 1)
                    dve.tensor_tensor(drop[:, kk, :], shift[:, kp, :], shift[:, kk, :], ALU.subtract).then_inc(s_drop, 1)

                def add_sums(j):
                    t = tile(-2, j)
                    a = acc[0:WN, bass.ds(win_at(pack, j) * (H * HF), H * HF)]
                    dve.wait_ge(s_decayed, sbn(-1)) if j == 0 else dve.wait_ge(s_acc, t)
                    dve.wait_ge(s_agg, t + 1)
                    dve.tensor_tensor(a, a, psum[0:WN, 4 + j % 2, 0:H * HF], ALU.add).then_inc(s_acc, 1)

                def decay_sums():
                    a = acc[0:WN, bass.ds(win_at(pack, 0) * (H * HF), H * HF)].rearrange("p (h f) -> p h f", h=H)
                    dve.wait_ge(s_decay, sbn(-1))
                    since(dve, s_acc, tile(-2, 0))
                    dve.tensor_tensor(a, a, decay[0:WN, (k - 2) % SPB, :].unsqueeze(2).to_broadcast([WN, H, HF]), ALU.mult)\
                       .then_inc(s_decayed, 1)

                def onehots():
                    oo = (k + 2) % SPB * SB
                    dve.wait_ge(s_rec, sbn(2) + 1)
                    if live(i, k, -2):
                        dve.wait_ge(s_agg, tile(-2, SB - 1) + 1)
                    dve.tensor_tensor(onehot[:, oo:oo + SB, 0:WN], iota_row[:, :].unsqueeze(1).to_broadcast([P, SB, WN]),
                                      rec[:, oo:oo + SB, 0:1].to_broadcast([P, SB, WN]), ALU.is_equal)
                    dve.tensor_copy(onehot[:, oo:oo + SB, WN:P], rec_b[:, oo:oo + SB, 2:5]).then_inc(s_onehot, 1)

                after = [[[(-1, bias)], [(-1, leaky)], [(-1, tiles_max), (-2, decay_sums)], [(-2, add_sums, 0)]],
                         [[(-1, heads_max)], [(-1, diagonal)], [(-2, add_sums, 1)], [(-1, new_shift)]],
                         [[(-1, shifted)], [(-2, add_sums, 2)], [(2, onehots)], []],
                         [[], [(-2, add_sums, 3)], [], []]]
                for j in range(SB):
                    for h in range(H):
                        if live(i, k, 0):
                            slot = k * SB + j
                            if h == 0:
                                dve.wait_ge(s_gather[slot], i * 16 + 16)
                            own = z_t[:, slot, h * AT:(h + 1) * AT]
                            op = dve.scalar_tensor_tensor(out=own, in0=own, scalar=0.0,
                                                          in1=a2_b[:, h * AT:(h + 1) * AT], op0=ALU.max, op1=ALU.mult,
                                                          accum_out=e_raw[:, slot, h:h + 1])
                            if h == H - 1:
                                op.then_inc(s_dot, 1)
                        for off, work, *args in after[j][h]:
                            if live(i, k, off):
                                work(*args)

            pipeline(dve, step)

            dve.wait_ge(s_acc, NT)
            dve.wait_ge(s_shift_all, NSB)
            dve.tensor_copy(c_last[:, :], last_sb[:, :]).then_inc(s_c_last, 1)
            dve.wait_ge(s_c_shifts, 32)
            dve.tensor_tensor(c_shift[0:SC], c_shift[0:SC], shift_all[0:SC, NSB - 1:NSB, :].to_broadcast([SC, KS, H]), ALU.subtract)\
               .then_inc(s_c_diff, 1)
            dve.wait_ge(s_c_last, 1)
            dve.wait_ge(s_c_const, 2)
            for k in range(KS):
                dve.tensor_scalar(c_oh[0:SC, k, :], c_last[0:SC, :], c_id[0:SC, k:k + 1], None, ALU.is_equal).then_inc(s_c_onehot, 1)
            dve.wait_ge(s_c_onehot, KS)
            dve.wait_ge(s_c_exp, 1)
            for k in range(KS):
                dve.tensor_tensor(c_pick[0:SC, k, :, :], c_oh[0:SC, k, :].unsqueeze(2).to_broadcast([SC, W, H]),
                                  c_exp[0:SC, k, :].unsqueeze(1).to_broadcast([SC, W, H]), ALU.mult).then_inc(s_c_pick, 1)
            dve.wait_ge(s_c_factor, 1)
            dve.tensor_copy(c_s[0:WN], psum[0:WN, 0, 0:W * H].rearrange("p (w h) -> p w h", w=W)).then_inc(s_c_coef, 1)
            dve.wait_ge(s_c_coef, 1)
            dve.tensor_tensor(c_d[0:WN], acc_w[0:WN].rearrange("p w (h f) -> p w h f", f=HF)[:, :, :, DO], c_s[0:WN], ALU.mult).then_inc(s_c_coef, 1)
            dve.wait_ge(s_c_coef, 2)
            dve.tensor_scalar(c_d[0:WN], c_d[0:WN], 1e-10, None, ALU.add).then_inc(s_c_coef, 1)
            dve.wait_ge(s_c_coef, 3)
            dve.reciprocal(c_k[0:WN], c_d[0:WN]).then_inc(s_c_coef, 1)
            dve.wait_ge(s_c_coef, 4)
            dve.tensor_tensor(c_k[0:WN], c_k[0:WN], c_s[0:WN], ALU.mult).then_inc(s_c_coef, 1)
            dve.wait_ge(s_c_coef, 5)

            def finish(i, k):
                g = i * CR + k
                if live_c(i, k, 0):
                    a4 = acc_w[0:WN, bass.ds(g * CG, CG), :].rearrange("p w (h f) -> p w h f", f=HF)
                    since(dve, s_c_ready, g - CR + 1)
                    dve.tensor_tensor(c_y[0:WN, k, :, :].rearrange("p w (h d) -> p w h d", h=H), a4[:, :, :, 0:DO],
                                      c_k[0:WN, bass.ds(g * CG, CG), :].unsqueeze(3).to_broadcast([WN, CG, H, DO]), ALU.mult)\
                       .then_inc(s_c_y, 1)
                if live_c(i, k, -1):
                    b = (k - 1) % CR
                    dve.wait_ge(s_c_add, g)
                    for v in range(CG):
                        op = dve.bn_stats(c_st[0:WN, b, v, :], c_y[0:WN, b, v, :])
                    op.then_inc(s_c_stats, 1)
                if live_c(i, k, -2):
                    b = (k - 2) % CR
                    dve.wait_ge(s_c_std, g - 1)
                    dve.reciprocal(c_is[0:WN, b, :], c_sd[0:WN, b, :]).then_inc(s_c_inv, 1)
                if live_c(i, k, -1):
                    b = (k - 1) % CR
                    dve.wait_ge(s_c_stats, g)
                    dve.sem_inc(s_passed_c, 1)
                    for v in range(CG):
                        op = dve.bn_aggr(c_mv[0:WN, b, v, :], c_st[0:WN, b, v, :])
                    op.then_inc(s_c_var, 1)
                if live_c(i, k, -2):
                    b = (k - 2) % CR
                    dve.wait_ge(s_c_inv, g - 1)
                    dve.scalar_tensor_tensor(out=c_nb[0:WN, b, :], in0=c_mv[0:WN, b, :, 0], scalar=-1.0, in1=c_is[0:WN, b, :],
                                             op0=ALU.mult, op1=ALU.mult).then_inc(s_c_bias, 1)

            finish_pipeline(dve, finish)


_INS = ["x", "src", "dst", "edge_weight", "L0_gnn_W1", "L0_gnn_b1", "L0_gnn_W2", "L0_gnn_b2",
        "L0_gnn_A1", "L0_gnn_ab1", "L0_gnn_A2", "L0_gnn_ab2"]


def kernel(**inputs):
    import numpy as _np
    import concourse.bacc as _bacc
    from concourse import mybir as _mybir
    from concourse.bass_utils import run_bass_kernel_spmd as _run

    nc = _bacc.Bacc("TRN2", target_bir_lowering=False, num_devices=1)
    arrays, args = {}, []
    for name in _INS:
        a = _np.ascontiguousarray(inputs[name])
        arrays[f"in_{name}_dram"] = a
        args.append(nc.dram_tensor(f"in_{name}_dram", a.shape, _mybir.dt.from_np(a.dtype), kind="ExternalInput").ap())
    args.append(nc.dram_tensor("out_0_dram", arrays["in_x_dram"].shape, _mybir.dt.float32, kind="ExternalOutput").ap())
    gnn_layer(nc, *args)
    r = _run(nc, [arrays], core_ids=[0])
    return r.results[0]["out_0_dram"]
```
